# Optimizing a Trainium2 kernel written in Bass

```python
import numpy as np
import jax
import jax.numpy as jnp

def _softmax(x, axis=-1):
    return jax.nn.softmax(x, axis=axis)

def _gelu(x):
    return jax.nn.gelu(x, approximate=True)

def _silu(x):
    return jax.nn.silu(x)

def _sigmoid(x):
    return jax.nn.sigmoid(x)

def _layernorm(x, axis=-1, eps=1e-05):
    m = jnp.mean(x, axis=axis, keepdims=True)
    v = jnp.var(x, axis=axis, keepdims=True)
    return (x - m) / jnp.sqrt(v + eps)

def _scatter_add(tgt, idx, src, axis=0):
    return tgt.at[idx].add(src)

def _segment_sum(src, seg, n):
    return jax.ops.segment_sum(src, seg, n)
kernel_name = 'mk_adj_ffn_d2_adj_r2_6b20e5'

def setup_inputs(seed: int=0):
    np.random.seed(seed)
    _w = jnp.asarray

    def _rec_inputs():
        import jax
        import jax.numpy as jnp
        _gk = jax.random.key(seed)
        x = -0.0003929 + 0.9999 * jax.random.normal(jax.random.fold_in(_gk, 1), (16, 512, 256), jnp.float32)
        _a = jax.random.bernoulli(jax.random.fold_in(_gk, 2), 0.015625, (16, 512, 512))
        _a = jnp.logical_or(_a, jnp.swapaxes(_a, -1, -2))
        _a = jnp.logical_or(_a, jnp.eye(512, dtype=bool))
        _af = _a.astype(jnp.float32)
        _af = _af * jax.random.uniform(jax.random.fold_in(_gk, 3), (16, 512, 512), jnp.float32, 0.05, 1)
        adj = _af
        return (x, adj)
    x, adj = _rec_inputs()

    def _L0_gnn_setup():
        import jax, jax.numpy as jnp
        import numpy as np
        B, N, F_IN, F_HID, F_OUT = (32, 512, 256, 256, 256)

        def _gcn_layer(x, adj, W, b):
            support = jnp.einsum('bnf,fh->bnh', x, W)
            return jnp.einsum('bnm,bmh->bnh', adj, support) + b
        key = jax.random.key(seed)
        ks = jax.random.split(key, 8)

        def xavier(k, fan_in, fan_out):
            bound = float(np.sqrt(6.0 / (fan_in + fan_out)))
            return jax.random.uniform(k, (fan_in, fan_out), jnp.float32, -bound, bound)
        return {'batch_graph': jax.random.normal(ks[0], (B, N, F_IN), jnp.float32), 'adj': jax.random.uniform(ks[1], (B, N, N), jnp.float32), 'W1': xavier(ks[2], F_IN, F_HID), 'b1': jnp.zeros((F_HID,), jnp.float32), 'W2': xavier(ks[3], F_HID, F_HID), 'b2': jnp.zeros((F_HID,), jnp.float32), 'W3': xavier(ks[4], F_HID, F_OUT), 'b3': jnp.zeros((F_OUT,), jnp.float32)}
    _L0_gnn_all = _L0_gnn_setup()
    _L0_gnn_in = {k: v for k, v in _L0_gnn_all.items() if k in ('W1', 'b1', 'W2', 'b2', 'W3', 'b3')}
    del _L0_gnn_all

    def _L0_ffn_setup():
        import jax, jax.numpy as jnp
        import numpy as np
        B, S, D, H, E = (4, 1024, 256, 512, 8)
        key = jax.random.key(seed)
        ks = jax.random.split(key, 4)
        x = jax.random.normal(ks[0], (B, S, D), jnp.float32)
        Wr = jax.random.normal(ks[1], (E, D), jnp.float32) * 0.02
        br = jnp.zeros((E,), jnp.float32)
        W1 = jax.random.normal(ks[2], (E, D, H), jnp.float32) * 0.02
        b1 = jnp.zeros((E, H), jnp.float32)
        W2 = jax.random.normal(ks[3], (E, H, D), jnp.float32) * 0.02
        b2 = jnp.zeros((E, D), jnp.float32)
        return {'x': x, 'Wr': Wr, 'br': br, 'W1': W1, 'b1': b1, 'W2': W2, 'b2': b2}
    _L0_ffn_all = _L0_ffn_setup()
    _L0_ffn_in = {k: v for k, v in _L0_ffn_all.items() if k in ('Wr', 'br', 'W1', 'b1', 'W2', 'b2')}
    del _L0_ffn_all

    def _L1_gnn_setup():
        import jax, jax.numpy as jnp
        import numpy as np
        B, N, DIN, DOUT, H = (32, 512, 256, 256, 8)
        DH = DOUT // H
        key = jax.random.key(seed)
        k1, k2, k3, k4, k5 = jax.random.split(key, 5)
        X = jax.random.normal(k1, (B, N, DIN), dtype=jnp.float32)
        A = (jax.random.uniform(k2, (B, N, N)) < 0.05).astype(jnp.float32)
        A = jnp.maximum(A, jnp.eye(N, dtype=jnp.float32)[None])
        std_w = np.sqrt(2.0 / (DIN + DH))
        std_c = np.sqrt(2.0 / (DH + DH))
        Wp = jax.random.normal(k3, (H, DIN, DH), dtype=jnp.float32) * std_w
        bp = jnp.zeros((H, DH), dtype=jnp.float32)
        C = jax.random.normal(k4, (H, DH, DH), dtype=jnp.float32) * std_c
        return {'X': X, 'A': A, 'Wp': Wp, 'bp': bp, 'C': C}
    _L1_gnn_all = _L1_gnn_setup()
    _L1_gnn_in = {k: v for k, v in _L1_gnn_all.items() if k in ('Wp', 'bp', 'C')}
    del _L1_gnn_all

    def _L1_ffn_setup():
        import jax, jax.numpy as jnp
        import numpy as np
        E = 64
        K = 2
        D = 256
        H = 128
        NSH = 2
        ROUTE_SCALE = 2.5
        CAP = 512
        STD = 0.02
        key = jax.random.key(seed)
        ks = jax.random.split(key, 8)
        x = jax.random.normal(ks[0], (4, 1024, D), dtype=jnp.float32)
        gate_w = jax.random.normal(ks[1], (E, D), dtype=jnp.float32) * STD
        w1 = jax.random.normal(ks[2], (E, D, H), dtype=jnp.float32) * STD
        w3 = jax.random.normal(ks[3], (E, D, H), dtype=jnp.float32) * STD
        w2 = jax.random.normal(ks[4], (E, H, D), dtype=jnp.float32) * STD
        sw1 = jax.random.normal(ks[5], (D, H * NSH), dtype=jnp.float32) * STD
        sw3 = jax.random.normal(ks[6], (D, H * NSH), dtype=jnp.float32) * STD
        sw2 = jax.random.normal(ks[7], (H * NSH, D), dtype=jnp.float32) * STD
        return {'x': x, 'gate_w': gate_w, 'w1': w1, 'w3': w3, 'w2': w2, 'sw1': sw1, 'sw3': sw3, 'sw2': sw2}
    _L1_ffn_all = _L1_ffn_setup()
    _L1_ffn_in = {k: v for k, v in _L1_ffn_all.items() if k in ('gate_w', 'w1', 'w3', 'w2', 'sw1', 'sw3', 'sw2')}
    del _L1_ffn_all
    return {'x': x, 'adj': adj, 'L0_gnn_W1': _L0_gnn_in['W1'], 'L0_gnn_b1': _L0_gnn_in['b1'], 'L0_gnn_W2': _L0_gnn_in['W2'], 'L0_gnn_b2': _L0_gnn_in['b2'], 'L0_gnn_W3': _L0_gnn_in['W3'], 'L0_gnn_b3': _L0_gnn_in['b3'], 'L0_ffn_Wr': _L0_ffn_in['Wr'], 'L0_ffn_br': _L0_ffn_in['br'], 'L0_ffn_W1': _L0_ffn_in['W1'], 'L0_ffn_b1': _L0_ffn_in['b1'], 'L0_ffn_W2': _L0_ffn_in['W2'], 'L0_ffn_b2': _L0_ffn_in['b2'], 'L1_gnn_Wp': _L1_gnn_in['Wp'], 'L1_gnn_bp': _L1_gnn_in['bp'], 'L1_gnn_C': _L1_gnn_in['C'], 'L1_ffn_gate_w': _L1_ffn_in['gate_w'], 'L1_ffn_w1': _L1_ffn_in['w1'], 'L1_ffn_w3': _L1_ffn_in['w3'], 'L1_ffn_w2': _L1_ffn_in['w2'], 'L1_ffn_sw1': _L1_ffn_in['sw1'], 'L1_ffn_sw3': _L1_ffn_in['sw3'], 'L1_ffn_sw2': _L1_ffn_in['sw2']}

def reference(x, adj, L0_gnn_W1, L0_gnn_b1, L0_gnn_W2, L0_gnn_b2, L0_gnn_W3, L0_gnn_b3, L0_ffn_Wr, L0_ffn_br, L0_ffn_W1, L0_ffn_b1, L0_ffn_W2, L0_ffn_b2, L1_gnn_Wp, L1_gnn_bp, L1_gnn_C, L1_ffn_gate_w, L1_ffn_w1, L1_ffn_w3, L1_ffn_w2, L1_ffn_sw1, L1_ffn_sw3, L1_ffn_sw2):
    import jax
    import jax.numpy as jnp

    def _L0_gnn_ref(batch_graph, adj, W1, b1, W2, b2, W3, b3):
        import jax, jax.numpy as jnp
        import numpy as np
        B, N, F_IN, F_HID, F_OUT = (32, 512, 256, 256, 256)

        def _gcn_layer(x, adj, W, b):
            support = jnp.einsum('bnf,fh->bnh', x, W)
            return jnp.einsum('bnm,bmh->bnh', adj, support) + b
        x = jax.nn.relu(_gcn_layer(batch_graph, adj, W1, b1))
        x = jax.nn.relu(_gcn_layer(x, adj, W2, b2))
        out = _gcn_layer(x, adj, W3, b3)
        return out

    def _L0_ffn_ref(x, Wr, br, W1, b1, W2, b2):
        import jax, jax.numpy as jnp
        import numpy as np
        B, S, D, H, E = (4, 1024, 256, 512, 8)
        b, s, d = x.shape
        n = b * s
        e = Wr.shape[0]
        xf = x.reshape(n, d)
        logits = xf @ Wr.T + br
        probs = jax.nn.softmax(logits, axis=-1)
        top2_prob, top2_idx = jax.lax.top_k(probs, 2)
        comb = jnp.zeros((n, e), x.dtype).at[jnp.arange(n)[:, None], top2_idx].add(top2_prob)
        h = jax.nn.gelu(jnp.einsum('nd,edh->enh', xf, W1) + b1[:, None, :], approximate=False)
        o = jnp.einsum('enh,ehd->end', h, W2) + b2[:, None, :]
        y = jnp.einsum('ne,end->nd', comb, o)
        return y.reshape(b, s, d)

    def _L1_gnn_ref(X, A, Wp, bp, C):
        import jax, jax.numpy as jnp
        import numpy as np
        B, N, DIN, DOUT, H = (32, 512, 256, 256, 8)
        DH = DOUT // H
        Xp = jnp.einsum('bnd,hdk->bhnk', X, Wp) + bp[None, :, None, :]
        Xc = jnp.einsum('bhnk,hjk->bhnj', Xp, C)
        attn = jnp.tanh(A[:, None] * jnp.einsum('bhnj,bhmj->bhnm', Xc, Xp))
        Xh = jnp.einsum('bhnm,bhmk->bhnk', attn, Xp)
        out = jnp.moveaxis(Xh, 1, 2).reshape(X.shape[0], X.shape[1], -1)
        return jax.nn.relu(out)

    def _L1_ffn_ref(x, gate_w, w1, w3, w2, sw1, sw3, sw2):
        import jax, jax.numpy as jnp
        import numpy as np
        E = 64
        K = 2
        D = 256
        H = 128
        NSH = 2
        ROUTE_SCALE = 2.5
        CAP = 512
        STD = 0.02
        bs, slen, d = x.shape
        xf = x.reshape(-1, d)
        logits = xf @ gate_w.T
        scores = jax.nn.sigmoid(logits.astype(jnp.float32))
        top_scores, top_idx = jax.lax.top_k(scores, K)
        top_scores = top_scores / (top_scores.sum(-1, keepdims=True) + 1e-20)
        top_scores = top_scores * ROUTE_SCALE
        flat_e = top_idx.reshape(-1)
        x_pairs = jnp.repeat(xf, K, axis=0)
        oh = jax.nn.one_hot(flat_e, E, dtype=jnp.int32)
        pos = jnp.take_along_axis(jnp.cumsum(oh, axis=0), flat_e[:, None], axis=1)[:, 0] - 1
        buf = jnp.zeros((E, CAP, d), dtype=xf.dtype).at[flat_e, pos].set(x_pairs, mode='drop')
        h = jax.nn.silu(jnp.einsum('ecd,edh->ech', buf, w1)) * jnp.einsum('ecd,edh->ech', buf, w3)
        y = jnp.einsum('ech,ehd->ecd', h, w2)
        valid = (pos < CAP)[:, None]
        y_pairs = jnp.where(valid, y[flat_e, jnp.minimum(pos, CAP - 1)], 0.0)
        routed = (y_pairs.reshape(-1, K, d) * top_scores[..., None].astype(xf.dtype)).sum(axis=1)
        shared = jax.nn.silu(xf @ sw1) * (xf @ sw3) @ sw2
        return (shared + routed).reshape(bs, slen, d)
    x = x + _L0_gnn_ref(_layernorm(x, axis=-1), adj, L0_gnn_W1, L0_gnn_b1, L0_gnn_W2, L0_gnn_b2, L0_gnn_W3, L0_gnn_b3)
    x = x + _L0_ffn_ref(_layernorm(x, axis=-1), L0_ffn_Wr, L0_ffn_br, L0_ffn_W1, L0_ffn_b1, L0_ffn_W2, L0_ffn_b2)
    x = x + _L1_gnn_ref(_layernorm(x, axis=-1), adj, L1_gnn_Wp, L1_gnn_bp, L1_gnn_C)
    x = x + _L1_ffn_ref(_layernorm(x, axis=-1), L1_ffn_gate_w, L1_ffn_w1, L1_ffn_w3, L1_ffn_w2, L1_ffn_sw1, L1_ffn_sw3, L1_ffn_sw2)
    return x

_drawn_inputs = setup_inputs


def setup_inputs(seed=0):
    import zlib

    import numpy as np

    out = dict(_drawn_inputs(seed))
    spreads = {'L0_gnn_b1': (0.0, 0.1),
     'L0_gnn_b2': (0.0, 0.682),
     'L0_gnn_b3': (0.0, 0.8),
     'L0_ffn_br': (0.0, 0.8),
     'L0_ffn_b1': (0.0, 0.8),
     'L0_ffn_b2': (0.0, 2.0),
     'L1_gnn_bp': (0.0, 0.272)}
    factors = {'L0_ffn_Wr': 8.0,
     'L0_ffn_W1': 8.0,
     'L0_ffn_W2': 8.0,
     'L1_ffn_gate_w': 8.0,
     'L1_ffn_w1': 8.0,
     'L1_ffn_w3': 8.0,
     'L1_ffn_w2': 8.0,
     'L1_ffn_sw1': 8.0,
     'L1_ffn_sw3': 8.0,
     'L1_ffn_sw2': 8.0}
    for name, (base, spread) in spreads.items():
        noise = np.random.default_rng([zlib.crc32(name.encode()), seed]).standard_normal(out[name].shape)
        drawn = base * np.exp(spread * noise) if base else spread * noise
        out[name] = jnp.asarray(drawn.astype(out[name].dtype))
    for name, factor in factors.items():
        out[name] = (out[name] * factor).astype(out[name].dtype)
    return out
```

```python
from contextlib import ExitStack

import numpy as np

import concourse.bass as bass
from concourse import mybir

F32 = mybir.dt.float32
BF16 = mybir.dt.bfloat16
I32 = mybir.dt.int32
U32 = mybir.dt.uint32
ALU = mybir.AluOpType
ACT = mybir.ActivationFunctionType
AX = mybir.AxisListType.X

P = 128
B, N, D = 16, 512, 256
T = N // P
TB = T // 2
KD = D // P
TOK = B * N

E0, H0 = 8, 512
KH0 = H0 // P
BLK = 512
REGION = TOK + BLK
SPARE = E0 * REGION
NBLK = 2 * TOK // BLK + E0
NTHR = TOK // BLK
PAIRS = 2 * TOK // P

HEADS, DH = 8, 32
GRP = 2
HG = HEADS // GRP

E1, H1, CAP = 64, 128, 512
HS = 256
KHS = HS // P
ROUTE_SCALE = 2.5
SKIP = float(1 << 20)

EPS = 1e-5

C_ID, C_TRI, C_ONE, C_IOTA, C_THR, C_BLK, C_END = np.cumsum([0, P, P, P, E1, NTHR, NBLK])
W1_0, W2_0, B1_0, W_END0 = np.cumsum([0, KD * H0, KH0 * D, KH0])
W1_1, W3_1, W2_1, W_END1 = np.cumsum([0, KD * H1, KD * H1, D])


def pairs(eng, n, body):
    body(0, 0, True, False)
    body(0, 1, False, n == 2)
    if n > 4:
        with eng.Fori(1, n // 2 - 1) as q:
            body(q, 0, False, False)
            body(q, 1, False, False)
    if n > 2:
        body(n // 2 - 1, 0, False, False)
        body(n // 2 - 1, 1, False, True)


def build(nc, a, out):
    with ExitStack() as whole:
        def sb(ctx, name, shape, dt=F32):
            return ctx.enter_context(nc.sbuf_tensor(name, shape, dt))

        x = sb(whole, "x", [P, B * T, D])
        consts = sb(whole, "consts", [P, C_END])
        tri = sb(whole, "tri", [P, P], BF16)
        ones = sb(whole, "ones", [P, P], BF16)
        half = sb(whole, "half", [P, T])
        zeros = sb(whole, "zeros", [P, T * D])
        adj = sb(whole, "adj", [P, 2, T, N])
        slot0 = sb(whole, "slot0", [P, PAIRS])
        rows0 = sb(whole, "rows0", [P, PAIRS], U32)
        gate0 = sb(whole, "gate0", [P, PAIRS])
        rows1 = sb(whole, "rows1", [P, PAIRS], U32)
        gate1 = sb(whole, "gate1", [P, PAIRS])
        count0 = sb(whole, "count0", [P, E0])
        count1 = sb(whole, "count1", [P, E1])
        ident = consts[:, C_ID:C_ID + P]

        moe0_in = nc.dram_tensor("moe0_in", [SPARE + BLK, D], F32).ap()
        moe0_out = nc.dram_tensor("moe0_out", [NBLK * BLK, D], F32).ap()
        moe1_in = nc.dram_tensor("moe1_in", [E1 * CAP, D], F32).ap()
        moe1_out = nc.dram_tensor("moe1_out", [E1 * CAP, D], F32).ap()

        m = dict(x=x, consts=consts, tri=tri, ones=ones, half=half, zeros=zeros, adj=adj, rows0=rows0,
                 gate0=gate0, rows1=rows1, gate1=gate1, count0=count0, count1=count1, ident=ident, slot0=slot0,
                 moe0_in=moe0_in, moe0_out=moe0_out, moe1_in=moe1_in, moe1_out=moe1_out)
        gcn_phase(nc, a, m, sb)
        moe0_phase(nc, a, m, sb)
        attention_phase(nc, a, m, sb)
        moe1_phase(nc, a, m, sb)
        combine_phase(nc, a, m, sb, out)


def own_wait(eng, mark):
    eng.sem_inc(mark, 1)


def transposes(pe, dst, src, ident, ready):
    for k in range(KD):
        for t in range(T):
            mm = pe.transpose(dst[:, k, t * P:(t + 1) * P], src[:, t, k * P:(k + 1) * P], ident)
    mm.then_inc(ready, 1)


def norm_stats(dve, x, b, stats, mv, step, at, mark):
    own_wait(dve, mark)
    for t in range(T):
        ins = dve.bn_stats(stats[:, t, :], x[:, b * T + t, :])
    ins.then_inc(step, 1)
    dve.wait_ge(step, at + 1)
    own_wait(dve, mark)
    for t in range(T):
        ins = dve.bn_aggr(mv[:, t, :], stats[:, t, :])
    ins.then_inc(step, 1)


def norm_scale(pool, mv, half, rstd, step, at, mark):
    own_wait(pool, mark)
    pool.tensor_scalar(rstd[:], mv[:, :, 1], EPS, None, ALU.add).then_inc(step, 1)
    pool.wait_ge(step, at + 1)
    pool.tensor_tensor(rstd[:], rstd[:], half[:], ALU.pow).then_inc(step, 1)


def norm_apply(dve, x, b, mv, rstd, xn, ready):
    for t in range(T):
        ins = dve.tensor_scalar(xn[:, t, :], x[:, b * T + t, :], mv[:, t, 0:1], rstd[:, t:t + 1],
                                ALU.subtract, ALU.mult)
    ins.then_inc(ready, 1)


def gcn_phase(nc, a, m, sb):
    x, adj, ident = m["x"], m["adj"], m["ident"]
    with ExitStack() as ctx:
        def sem(name):
            return ctx.enter_context(nc.semaphore("a_" + name))

        mark_dve, mark_pool, mark_sp = sem("mark_dve"), sem("mark_pool"), sem("mark_sp")

        def psum(name, shape):
            return ctx.enter_context(nc.psum_tensor("a_" + name, shape, F32))

        w = sb(ctx, "a_w", [P, 3, KD, D])
        bias = sb(ctx, "a_bias", [P, 2, KD])
        bias3 = sb(ctx, "a_bias3", [P, D])
        wr = sb(ctx, "a_wr", [P, KD, E0])
        br = sb(ctx, "a_br", [P, E0])
        feat = sb(ctx, "a_feat", [P, KD, N])
        sup = sb(ctx, "a_sup", [P, T, D])
        xn1 = sb(ctx, "a_xn1", [P, T, D])
        xn2 = sb(ctx, "a_xn2", [P, 2, T, D])
        xt2 = sb(ctx, "a_xt2", [P, KD, N])
        st1, mv1, rs1 = sb(ctx, "a_st1", [P, T, 6]), sb(ctx, "a_mv1", [P, T, 2]), sb(ctx, "a_rs1", [P, T])
        st2, mv2, rs2 = sb(ctx, "a_st2", [P, T, 6]), sb(ctx, "a_mv2", [P, T, 2]), sb(ctx, "a_rs2", [P, T])
        lg = sb(ctx, "a_lg", [P, T, E0])
        mx = sb(ctx, "a_mx", [P, T])
        ex = sb(ctx, "a_ex", [P, T, E0])
        sm = sb(ctx, "a_sm", [P, 2, T])
        pr = sb(ctx, "a_pr", [P, T, E0])
        top = sb(ctx, "a_top", [P, T, 8])
        idx = sb(ctx, "a_idx", [P, T, 8], U32)
        idf = sb(ctx, "a_idf", [P, 2, T])
        oh = sb(ctx, "a_oh", [P, 2, T, E0])
        member = sb(ctx, "a_member", [P, T + 1, E0], BF16)
        pos = sb(ctx, "a_pos", [P, T, E0])
        own = sb(ctx, "a_own", [P, 2, T, E0])
        ownpos = sb(ctx, "a_ownpos", [P, 2, T])
        rows = sb(ctx, "a_rows", [P, 2, 2, T], U32)

        p_agg = psum("p_agg", [P, 2, 512])
        p_sup = psum("p_sup", [P, T, D])
        p_tr = psum("p_tr", [P, KD, N])
        p_log = psum("p_log", [P, 512])
        p_pos = psum("p_pos", [P, 512])
        logit = p_log[:, 0:T * E0].rearrange("p (t e) -> p t e", t=T)
        count = p_pos[:, 0:(T + 1) * E0].rearrange("p (t e) -> p t e", t=T + 1)

        s_const, s_w, s_in = sem("const"), sem("w"), [sem("in0"), sem("in1")]
        init_dve, init_pool = sem("init_dve"), sem("init_pool")
        ln1_step, ln1_rs, xn1_ready = sem("ln1_step"), sem("ln1_rs"), sem("xn1_ready")
        ln2_step, ln2_rs, xn2_ready = sem("ln2_step"), sem("ln2_rs"), sem("xn2_ready")
        tr1_done, feat1_ready = sem("tr1_done"), sem("feat1_ready")
        tr2_done, xt2_ready = sem("tr2_done"), sem("xt2_ready")
        sup_done, sup_ready = sem("sup_done"), sem("sup_ready")
        agg_done, feat_ready = sem("agg_done"), sem("feat_ready")
        biased, x1_ready = sem("biased"), sem("x1_ready")
        log_done, lg_ready, ex_ready = sem("log_done"), sem("lg_ready"), sem("ex_ready")
        route_step, member_ready, count_done = sem("route_step"), sem("member_ready"), sem("count_done")
        rows_ready = sem("rows_ready")
        scattered = [sem("scattered0"), sem("scattered1")]
        s_zero = sem("zero")
        ROUTE_STEPS = 12

        block = ctx.enter_context(nc.Block())

        @block.sync
        def _(sp):
            sp.dma_start(m["consts"][:], a["consts"]).then_inc(s_const, 16)
            for dst, name in ((w[:, 0], "w1"), (w[:, 1], "w2"), (w[:, 2], "w3"), (bias[:, 0, :], "b1"),
                              (bias[:, 1, :], "b2"), (wr[:], "wr")):
                sp.dma_start(dst, a[name]).then_inc(s_w, 16)
            sp.dma_start(bias3[:], a["b3"].partition_broadcast(P)).then_inc(s_w, 16)
            sp.dma_start(br[:], a["br"].partition_broadcast(P)).then_inc(s_w, 16)
            sp.wait_ge(init_pool, 2)
            zero_rows = m["moe1_in"].rearrange("(i p t) d -> i p (t d)", p=P, t=T)
            def graph(q, h, first, last):
                b = 2 * q + h
                if not (first or (h == 1 and isinstance(q, int) and q == 0)):
                    sp.wait_ge(agg_done, 6 * (b - 1))
                sp.dma_start(adj[:, h], a["adj"][b]).then_inc(s_in[h], 16)
                sp.dma_start(x[:, bass.ds(b * T, T), :], a["x"][:, bass.ds(b * T, T), :])\
                  .then_inc(s_in[h], 16)
                for i in range(E1 // B):
                    sp.dma_start(zero_rows[b * (E1 // B) + i], m["zeros"][:]).then_inc(s_zero, 16)
            pairs(sp, B, graph)
            sp.dma_start(m["moe0_in"][SPARE:SPARE + BLK, :].rearrange("(p t) d -> p (t d)", p=P),
                         m["zeros"][:]).then_inc(s_zero, 16)
            sp.wait_ge(s_zero, 16 * (E1 + 1))

        @block.gpsimd
        def _(pool):
            pool.memset(m["half"][:], -0.5).then_inc(init_pool, 1)
            pool.memset(m["zeros"][:], 0.0).then_inc(init_pool, 1)
            pool.wait_ge(init_pool, 2)

            def scale1(b):
                pool.wait_ge(ln1_step, 2 * b + 2)
                norm_scale(pool, mv1, m["half"], rs1, ln1_rs, 2 * b, mark_pool)

            def scatter(q, h):
                b = 2 * q + h
                pool.wait_ge(rows_ready, b + 1)
                own_wait(pool, mark_pool)
                for k in range(2):
                    for t in range(T):
                        pool.indirect_dma_start(
                            out=m["moe0_in"], out_offset=bass.IndirectOffsetOnAxis(ap=rows[:, h, k, t:t + 1], axis=0),
                            in_=xn2[:, h, t, :], in_offset=None).then_inc(scattered[h], 16)

            def graph(q, h, first, last):
                b = 2 * q + h
                if not last:
                    scale1(b + 1)
                pool.wait_ge(xn1_ready, b + 1)
                if first:
                    pool.wait_ge(s_w, 16 * 8)
                for t in range(T):
                    ins = pool.tensor_tensor(x[:, b * T + t, :], x[:, b * T + t, :], bias3[:], ALU.add)
                ins.then_inc(biased, 1)
                if not first:
                    scatter(q - 1 + h, 1 - h)
                pool.wait_ge(ln2_step, 2 * b + 2)
                norm_scale(pool, mv2, m["half"], rs2, ln2_rs, 2 * b, mark_pool)

            scale1(0)
            pairs(pool, B, graph)
            scatter(B // 2 - 1, 1)
            for h in range(2):
                pool.wait_ge(scattered[h], 16 * 2 * T * (B // 2))

        @block.tensor
        def _(pe):
            def transpose_in(b, h):
                pe.wait_ge(xn1_ready, b + 1)
                transposes(pe, p_tr, xn1, ident, tr1_done)

            def support(b, layer):
                for t in range(T):
                    for k in range(KD):
                        mm = pe.matmul(p_sup[:, t, :], feat[:, k, t * P:(t + 1) * P], w[:, layer, k, :],
                                       start=(k == 0), stop=(k == KD - 1))
                    if t % 2:
                        mm.then_inc(sup_done, 1)

            def aggregate(b, layer, h):
                for f in range(KD):
                    for t in range(T):
                        if f == 0 and t % 2 == 0:
                            pe.wait_ge(sup_ready, 3 * TB * b + TB * layer + t // 2 + 1)
                        mm = pe.matmul(p_agg[:, f, :], sup[:, t, f * P:(f + 1) * P], adj[:, h, t, :],
                                       start=(t == 0), stop=(t == T - 1))
                    mm.then_inc(agg_done, 1)

            def aggregate_out(b, h):
                out = p_agg[:].rearrange("p a (c d) -> p (a c) d", d=D)
                pe.wait_ge(sup_ready, 3 * TB * b + 3 * TB)
                for n in range(T):
                    for t in range(T):
                        mm = pe.matmul(out[:, n, :], adj[:, h, t, n * P:(n + 1) * P], sup[:, t, :],
                                       start=(t == 0), stop=(t == T - 1))
                    if n % 2:
                        mm.then_inc(agg_done, 1)

            def route_logits(b):
                pe.wait_ge(xt2_ready, b + 1)
                for t in range(T):
                    for k in range(KD):
                        mm = pe.matmul(logit[:, t, :], xt2[:, k, t * P:(t + 1) * P], wr[:, k, :],
                                       start=(k == 0), stop=(k == KD - 1))
                mm.then_inc(log_done, 1)

            def route_counts(b):
                pe.wait_ge(member_ready, b + 1)
                count_before(pe, m, count, member, count_done)

            def graph(q, h, first, last):
                b = 2 * q + h
                pe.wait_ge(s_in[h], 32 * (q + 1))
                pe.wait_ge(feat1_ready, b + 1)
                if not first:
                    pe.wait_ge(x1_ready, TB * b)
                support(b, 0)
                aggregate(b, 0, h)
                if not first:
                    pe.wait_ge(xn2_ready, b)
                    transposes(pe, p_tr, xn2[:, 1 - h], ident, tr2_done)
                pe.wait_ge(feat_ready, 4 * b + 2)
                support(b, 1)
                if not first:
                    route_logits(b - 1)
                aggregate(b, 1, h)
                pe.wait_ge(feat_ready, 4 * b + 4)
                support(b, 2)
                aggregate_out(b, h)
                if not first:
                    route_counts(b - 1)
                if not last:
                    transpose_in(b + 1, 1 - h)

            pe.wait_ge(s_const, 16)
            pe.wait_ge(s_w, 16 * 8)
            pe.wait_ge(init_dve, 4)
            transpose_in(0, 0)
            pairs(pe, B, graph)
            pe.wait_ge(xn2_ready, B)
            transposes(pe, p_tr, xn2[:, 1], ident, tr2_done)
            route_logits(B - 1)
            route_counts(B - 1)

        @block.scalar
        def _(act):
            def evac_in(b):
                act.wait_ge(tr1_done, b + 1)
                act.activation(feat[:], p_tr[:], ACT.Copy).then_inc(feat1_ready, 1)

            def evac_support(b, layer):
                for c in range(TB):
                    act.wait_ge(sup_done, 3 * TB * b + TB * layer + c + 1)
                    act.activation(sup[:, 2 * c:2 * c + 2, :], p_sup[:, 2 * c:2 * c + 2, :], ACT.Copy)\
                       .then_inc(sup_ready, 1)

            def evac_layer(b, layer):
                for f in range(KD):
                    act.wait_ge(agg_done, 6 * b + 2 * layer + f + 1)
                    act.activation(feat[:, f, :], p_agg[:, f, :], ACT.Relu, bias=bias[:, layer, f:f + 1])\
                       .then_inc(feat_ready, 1)

            def evac_router(b):
                act.wait_ge(tr2_done, b + 1)
                act.activation(xt2[:], p_tr[:], ACT.Copy).then_inc(xt2_ready, 1)

            def exps(b):
                act.wait_ge(lg_ready, b + 1)
                act.activation(ex[:], lg[:], ACT.Exp).then_inc(ex_ready, 1)

            def graph(q, h, first, last):
                b = 2 * q + h
                evac_support(b, 0)
                evac_layer(b, 0)
                if not first:
                    evac_router(b - 1)
                evac_support(b, 1)
                evac_layer(b, 1)
                if not first:
                    exps(b - 1)
                evac_support(b, 2)
                if not last:
                    evac_in(b + 1)

            act.wait_ge(s_w, 16 * 8)
            evac_in(0)
            pairs(act, B, graph)
            evac_router(B - 1)
            exps(B - 1)

        @block.vector
        def _(dve):
            dve.wait_ge(s_const, 16)
            dve.tensor_copy(m["tri"][:], m["consts"][:, C_TRI:C_TRI + P]).then_inc(init_dve, 1)
            dve.tensor_copy(m["ones"][:], m["consts"][:, C_ONE:C_ONE + P]).then_inc(init_dve, 1)
            dve.memset(member[:], 0.0).then_inc(init_dve, 1)
            dve.memset(m["count0"][:], 0.0)
            dve.memset(m["count1"][:], 0.0).then_inc(init_dve, 1)
            dve.wait_ge(init_dve, 4)
            dve.wait_ge(s_w, 16 * 8)

            def norm1(q, h):
                b = 2 * q + h
                dve.wait_ge(s_in[h], 32 * (q + 1))
                norm_stats(dve, x, b, st1, mv1, ln1_step, 2 * b, mark_dve)
                dve.wait_ge(ln1_rs, 2 * b + 2)
                if not (isinstance(b, int) and b == 0):
                    dve.wait_ge(tr1_done, b)
                norm_apply(dve, x, b, mv1, rs1, xn1, xn1_ready)

            def residual_norm2(q, h):
                b = 2 * q + h
                out = p_agg[:].rearrange("p a (c d) -> p (a c) d", d=D)
                dve.wait_ge(biased, b + 1)
                for c in range(TB):
                    dve.wait_ge(agg_done, 6 * b + 4 + c + 1)
                    xc = x[:, bass.ds(b * T + 2 * c, 2), :]
                    dve.tensor_tensor(xc, xc, out[:, 2 * c:2 * c + 2, :], ALU.add).then_inc(x1_ready, 1)
                dve.wait_ge(x1_ready, TB * b + TB)
                norm_stats(dve, x, b, st2, mv2, ln2_step, 2 * b, mark_dve)
                dve.wait_ge(ln2_rs, 2 * b + 2)
                if not (isinstance(q, int) and q == 0):
                    dve.wait_ge(scattered[h], 16 * 2 * T * q)
                norm_apply(dve, x, b, mv2, rs2, xn2[:, h], xn2_ready)

            def route_choose(b):
                s = ROUTE_STEPS * b
                dve.wait_ge(log_done, b + 1)
                dve.tensor_tensor(lg[:], logit, br[:].unsqueeze(1).broadcast_to([P, T, E0]), ALU.add)\
                   .then_inc(route_step, 1)
                dve.wait_ge(route_step, s + 1)
                dve.tensor_reduce(mx[:], lg[:], AX, ALU.max).then_inc(route_step, 1)
                dve.wait_ge(route_step, s + 2)
                dve.tensor_tensor(lg[:], lg[:], mx[:].unsqueeze(2).broadcast_to([P, T, E0]), ALU.subtract)\
                   .then_inc(lg_ready, 1)
                dve.wait_ge(ex_ready, b + 1)
                dve.tensor_reduce(sm[:, 0, :], ex[:], AX, ALU.add).then_inc(route_step, 1)
                dve.wait_ge(route_step, s + 3)
                dve.reciprocal(sm[:, 1, :], sm[:, 0, :]).then_inc(route_step, 1)
                dve.wait_ge(route_step, s + 4)
                dve.tensor_tensor(pr[:], ex[:], sm[:, 1, :].unsqueeze(2).broadcast_to([P, T, E0]), ALU.mult)\
                   .then_inc(route_step, 1)
                dve.wait_ge(route_step, s + 5)
                own_wait(dve, mark_dve)
                for t in range(T):
                    ins = dve.max(top[:, t, :], pr[:, t, :])
                ins.then_inc(route_step, 1)
                dve.wait_ge(route_step, s + 6)
                own_wait(dve, mark_dve)
                for t in range(T):
                    ins = dve.max_index(idx[:, t, :], top[:, t, :], pr[:, t, :])
                ins.then_inc(route_step, 1)
                dve.wait_ge(route_step, s + 7)
                dve.tensor_copy(idf[:], idx[:, :, 0:2].rearrange("p t k -> p k t")).then_inc(route_step, 1)
                dve.tensor_copy(m["gate0"][:, bass.ds(b * 2 * T, 2 * T)].rearrange("p (k t) -> p k t", k=2),
                                top[:, :, 0:2].rearrange("p t k -> p k t"))
                dve.wait_ge(route_step, s + 8)
                iota = m["consts"][:, C_IOTA:C_IOTA + E0].unsqueeze(1).unsqueeze(1).broadcast_to([P, 2, T, E0])
                dve.tensor_tensor(oh[:], iota, idf[:].unsqueeze(3).broadcast_to([P, 2, T, E0]), ALU.is_equal)\
                   .then_inc(route_step, 1)
                dve.wait_ge(route_step, s + 9)
                dve.tensor_tensor(member[:, 0:T, :], oh[:, 0], oh[:, 1], ALU.add).then_inc(member_ready, 1)

            def route_rows(q, h):
                b = 2 * q + h
                s = ROUTE_STEPS * b
                dve.wait_ge(count_done, b + 1)
                dve.tensor_tensor(pos[:], count[:, 0:T, :], m["count0"][:].unsqueeze(1).broadcast_to([P, T, E0]),
                                  ALU.add).then_inc(route_step, 1)
                dve.wait_ge(route_step, s + 10)
                dve.tensor_tensor(m["count0"][:], m["count0"][:], count[:, T, :], ALU.add)
                dve.tensor_tensor(own[:], oh[:], pos[:].unsqueeze(1).broadcast_to([P, 2, T, E0]), ALU.mult)\
                   .then_inc(route_step, 1)
                dve.wait_ge(route_step, s + 11)
                dve.tensor_reduce(ownpos[:], own[:], AX, ALU.add).then_inc(route_step, 1)
                dve.wait_ge(route_step, s + 12)
                if not (isinstance(q, int) and q == 0):
                    dve.wait_ge(scattered[h], 16 * 2 * T * q)
                dve.scalar_tensor_tensor(out=rows[:, h], in0=idf[:], scalar=float(REGION), in1=ownpos[:],
                                         op0=ALU.mult, op1=ALU.add).then_inc(rows_ready, 1)
                dve.wait_ge(rows_ready, b + 1)
                dve.tensor_copy(m["slot0"][:, bass.ds(b * 2 * T, 2 * T)].rearrange("p (k t) -> p k t", k=2),
                                rows[:, h])

            def graph(q, h, first, last):
                if not last:
                    norm1(q + h, 1 - h)
                if not first:
                    route_choose(2 * q + h - 1)
                    route_rows(q - 1 + h, 1 - h)
                residual_norm2(q, h)

            norm1(0, 0)
            pairs(dve, B, graph)
            route_choose(B - 1)
            route_rows(B // 2 - 1, 1)


def count_before(pe, m, count, member, done):
    pe.matmul(count[:], m["tri"][:], member[:], start=True, stop=False, skip_group_check=True)
    for t in range(T):
        mm = pe.matmul(count[:, t + 1:T + 1, :], m["ones"][:],
                       member[:, t:t + 1, :].broadcast_to([P, T - t, member.shape[2]]),
                       start=False, stop=(t == T - 1), skip_group_check=True)
    mm.then_inc(done, 1)


def moe0_phase(nc, a, m, sb):
    ident = m["ident"]
    with ExitStack() as ctx:
        def sem(name):
            return ctx.enter_context(nc.semaphore("b_" + name))

        mark_dve, mark_pool, mark_sp = sem("mark_dve"), sem("mark_pool"), sem("mark_sp")

        def psum(name, shape):
            return ctx.enter_context(nc.psum_tensor("b_" + name, shape, F32))

        w = sb(ctx, "b_w", [P, 2, W_END0])
        b2 = sb(ctx, "b_b2", [P, 2, D])
        xin = sb(ctx, "b_xin", [P, 2, T, D])
        xt = sb(ctx, "b_xt", [P, KD, BLK])
        ht = sb(ctx, "b_ht", [P, KH0, BLK])
        y = sb(ctx, "b_y", [P, 2, T, D])
        over = sb(ctx, "b_over", [P, E0, NTHR])
        blocks = sb(ctx, "b_blocks", [P, 3, E0])
        shift = sb(ctx, "b_shift", [P, 2, E0])
        beyond = sb(ctx, "b_beyond", [P, PAIRS, E0])
        moved = sb(ctx, "b_moved", [P, PAIRS])
        past = sb(ctx, "b_past", [1, 2, NBLK, E0])
        expert = sb(ctx, "b_expert", [1, 4, NBLK])
        tail = sb(ctx, "b_tail", [1, E0])
        table = sb(ctx, "b_table", [1, 2, NBLK], I32)
        tails = sb(ctx, "b_tails", [1, E0], I32)

        p_tr = psum("p_tr", [P, KD, BLK])
        p_h = psum("p_h", [P, KH0, BLK])
        p_y = psum("p_y", [P, T, D])

        rows_out = m["moe0_out"].rearrange("(j p t) d -> j p (t d)", p=P, t=T)
        step, table_ready = sem("step"), sem("table")
        s_tail = sem("tail")
        s_rows, s_w = [sem("rows0"), sem("rows1")], [sem("w0"), sem("w1")]
        s_out = [sem("out0"), sem("out1")]
        tr_done, xt_ready, h_done, h_ready = sem("tr_done"), sem("xt_ready"), sem("h_done"), sem("h_ready")
        y_done, y_ready = sem("y_done"), sem("y_ready")

        block = ctx.enter_context(nc.Block())

        @block.vector
        def _(dve):
            c0 = m["count0"]
            thr = m["consts"][:, C_THR:C_THR + NTHR]
            blk = m["consts"][0:1, C_BLK:C_BLK + NBLK]
            dve.tensor_tensor(over[:], c0[:].unsqueeze(2).broadcast_to([P, E0, NTHR]),
                              thr.unsqueeze(1).broadcast_to([P, E0, NTHR]), ALU.is_gt).then_inc(step, 1)
            dve.scalar_tensor_tensor(out=tails[:], in0=m["consts"][0:1, C_IOTA:C_IOTA + E0],
                                     scalar=float(REGION), in1=c0[0:1, :],
                                     op0=ALU.mult, op1=ALU.add).then_inc(table_ready, 1)
            dve.memset(blocks[:, 2, :], 1.0)
            dve.wait_ge(step, 1)
            dve.tensor_reduce(blocks[:, 0, :], over[:], AX, ALU.add).then_inc(step, 1)
            dve.wait_ge(step, 2)
            dve.tensor_tensor_scan(blocks[:, 1, :], blocks[:, 2, :], blocks[:, 0, :], 0.0, ALU.mult, ALU.add)\
               .then_inc(step, 1)
            dve.wait_ge(step, 3)
            dve.tensor_tensor(past[:, 0], blocks[0:1, 1, :].unsqueeze(1).broadcast_to([1, NBLK, E0]),
                              blk.unsqueeze(2).broadcast_to([1, NBLK, E0]), ALU.is_le).then_inc(step, 1)
            dve.wait_ge(step, 4)
            dve.tensor_tensor(past[:, 1], past[:, 0], blocks[0:1, 0, :].unsqueeze(1).broadcast_to([1, NBLK, E0]),
                              ALU.mult)
            dve.tensor_reduce(expert[:, 0, :], past[:, 0], AX, ALU.add).then_inc(step, 1)
            dve.wait_ge(step, 5)
            dve.tensor_reduce(expert[:, 1, :], past[:, 1], AX, ALU.add).then_inc(step, 1)
            dve.wait_ge(step, 6)
            dve.tensor_tensor(expert[:, 2, :], blk, expert[:, 1, :], ALU.subtract).then_inc(step, 1)
            dve.wait_ge(step, 7)
            dve.tensor_scalar(expert[:, 3, :], expert[:, 2, :], float(BLK), None, ALU.mult).then_inc(step, 1)
            dve.wait_ge(step, 8)
            dve.scalar_tensor_tensor(out=expert[:, 1, :], in0=expert[:, 0, :], scalar=float(REGION),
                                     in1=expert[:, 3, :], op0=ALU.mult, op1=ALU.add).then_inc(step, 1)
            dve.wait_ge(step, 9)
            dve.tensor_scalar(table[:, 0, :], expert[:, 1, :], float(SPARE), None, ALU.min)\
               .then_inc(table_ready, 1)
            dve.tensor_scalar(table[:, 1, :], expert[:, 0, :], float(E0 - 1), None, ALU.min)\
               .then_inc(table_ready, 1)
            dve.tensor_scalar(shift[:, 0, :], m["consts"][:, C_IOTA:C_IOTA + E0], float(REGION), None, ALU.mult)\
               .then_inc(step, 1)
            dve.tensor_scalar(shift[:, 1, 1:E0], blocks[:, 0, 0:E0 - 1], float(BLK), -float(REGION),
                              ALU.mult, ALU.add)
            dve.memset(shift[:, 1, 0:1], 0.0).then_inc(step, 1)
            dve.wait_ge(step, 11)
            dve.tensor_tensor(beyond[:], m["slot0"][:].unsqueeze(2).broadcast_to([P, PAIRS, E0]),
                              shift[:, 0, :].unsqueeze(1).broadcast_to([P, PAIRS, E0]), ALU.is_ge).then_inc(step, 1)
            dve.wait_ge(step, 12)
            dve.tensor_tensor(beyond[:], beyond[:], shift[:, 1, :].unsqueeze(1).broadcast_to([P, PAIRS, E0]),
                              ALU.mult).then_inc(step, 1)
            dve.wait_ge(step, 13)
            dve.tensor_reduce(moved[:], beyond[:], AX, ALU.add).then_inc(step, 1)
            dve.wait_ge(step, 14)
            dve.tensor_tensor(m["rows0"][:], m["slot0"][:], moved[:], ALU.add)

            def one(q, h, first, last):
                j = 2 * q + h
                if not (isinstance(q, int) and q == 0):
                    dve.wait_ge(s_out[h], 16 * q)
                dve.wait_ge(s_w[h], 32 * (q + 1))
                for c in range(TB):
                    dve.wait_ge(y_done, TB * j + c + 1)
                    dve.tensor_tensor(y[:, h, 2 * c:2 * c + 2, :], p_y[:, 2 * c:2 * c + 2, :],
                                      b2[:, h, :].unsqueeze(1).broadcast_to([P, 2, D]), ALU.add).then_inc(y_ready, 1)
            pairs(dve, NBLK, one)

        @block.sync
        def _(sp):
            sp.wait_ge(table_ready, 3)
            for e in range(E0):
                row = sp.value_load(tails[0:1, e:e + 1], min_val=0, max_val=SPARE - BLK)
                sp.dma_start(m["moe0_in"][bass.ds(row, BLK), :].rearrange("(p t) d -> p (t d)", p=P),
                             m["zeros"][:]).then_inc(s_tail, 16)
            sp.wait_ge(s_tail, 16 * E0)

            def load_rows(q, h):
                row = sp.value_load(table[0:1, 0, bass.ds(2 * q + h, 1)], min_val=0, max_val=SPARE)
                sp.dma_start(xin[:, h].rearrange("p t d -> p (t d)"),
                             m["moe0_in"][bass.ds(row, BLK), :].rearrange("(p t) d -> p (t d)", p=P))\
                  .then_inc(s_rows[h], 16)

            def load_weights(q, h):
                e = sp.value_load(table[0:1, 1, bass.ds(2 * q + h, 1)], min_val=0, max_val=E0 - 1)
                sp.dma_start(w[:, h, :], a["moe0_w"][bass.ds(e, 1)].rearrange("e p c -> p (e c)"))\
                  .then_inc(s_w[h], 16)
                sp.dma_start(b2[:, h, :], a["moe0_b2"][bass.ds(e, 1)].rearrange("e d -> (e d)").partition_broadcast(P))\
                  .then_inc(s_w[h], 16)

            def one(q, h, first, last):
                j = 2 * q + h
                if first:
                    load_weights(0, 1)
                elif not last:
                    sp.wait_ge(y_ready, TB * j)
                    own_wait(sp, mark_sp)
                    load_weights(q + h, 1 - h)
                if not (last or (h == 0 and isinstance(q, int) and q == NBLK // 2 - 1)):
                    sp.wait_ge(tr_done, j + 1)
                    own_wait(sp, mark_sp)
                    load_rows(q + 1, h)
                sp.wait_ge(y_ready, TB * j + TB)
                sp.dma_start(rows_out[j],
                             y[:, h].rearrange("p t d -> p (t d)")).then_inc(s_out[h], 16)
            load_rows(0, 0)
            load_weights(0, 0)
            load_rows(0, 1)
            pairs(sp, NBLK, one)
            for h in range(2):
                sp.wait_ge(s_out[h], 16 * (NBLK // 2))

        @block.tensor
        def _(pe):
            def turn(q, h):
                pe.wait_ge(s_rows[h], 16 * (q + 1))
                transposes(pe, p_tr, xin[:, h], ident, tr_done)

            def one(q, h, first, last):
                j = 2 * q + h
                pe.wait_ge(s_w[h], 32 * (q + 1))
                pe.wait_ge(xt_ready, j + 1)
                for c in range(KH0):
                    for k in range(KD):
                        col = W1_0 + k * H0 + c * P
                        mm = pe.matmul(p_h[:, c, :], w[:, h, col:col + P], xt[:, k, :],
                                       start=(k == 0), stop=(k == KD - 1))
                    mm.then_inc(h_done, 1)
                if not last:
                    turn(q + h, 1 - h)
                for t in range(T):
                    if not first and t % 2 == 0:
                        pe.wait_ge(y_ready, TB * (j - 1) + t // 2 + 1)
                    for c in range(KH0):
                        if t == 0:
                            pe.wait_ge(h_ready, KH0 * j + c + 1)
                        mm = pe.matmul(p_y[:, t, :], ht[:, c, t * P:(t + 1) * P],
                                       w[:, h, W2_0 + c * D:W2_0 + (c + 1) * D],
                                       start=(c == 0), stop=(c == KH0 - 1))
                    if t % 2:
                        mm.then_inc(y_done, 1)
            turn(0, 0)
            pairs(pe, NBLK, one)

        @block.scalar
        def _(act):
            def evac(j):
                act.wait_ge(tr_done, j + 1)
                act.activation(xt[:], p_tr[:], ACT.Copy).then_inc(xt_ready, 1)

            def one(q, h, first, last):
                j = 2 * q + h
                for c in range(KH0):
                    act.wait_ge(h_done, KH0 * j + c + 1)
                    act.activation(ht[:, c, :], p_h[:, c, :], ACT.Gelu, bias=w[:, h, B1_0 + c:B1_0 + c + 1])\
                       .then_inc(h_ready, 1)
                if not last:
                    evac(j + 1)
            evac(0)
            pairs(act, NBLK, one)


def attention_phase(nc, a, m, sb):
    x, adj, ident = m["x"], m["adj"], m["ident"]
    with ExitStack() as ctx:
        def sem(name):
            return ctx.enter_context(nc.semaphore("c_" + name))

        mark_dve, mark_pool, mark_sp = sem("mark_dve"), sem("mark_pool"), sem("mark_sp")

        def psum(name, shape):
            return ctx.enter_context(nc.psum_tensor("c_" + name, shape, F32))

        wp = sb(ctx, "c_wp", [P, KD, D])
        bpc = sb(ctx, "c_bpc", [P, GRP])
        bpr = sb(ctx, "c_bpr", [P, D])
        cd = sb(ctx, "c_cd", [P, GRP, P])
        wg = sb(ctx, "c_wg", [P, KD, E1])
        ws1, ws3 = sb(ctx, "c_ws1", [P, KD, HS]), sb(ctx, "c_ws3", [P, KD, HS])
        ws2 = sb(ctx, "c_ws2", [P, KHS, D])
        g = sb(ctx, "c_g", [P, 2 * T, D])
        grow = sb(ctx, "c_grow", [P, 2 * T], U32)
        ggate = sb(ctx, "c_ggate", [P, 2 * T])
        xn = sb(ctx, "c_xn", [P, T, D])
        xn3 = sb(ctx, "c_xn3", [P, 2, T, D])
        xt = sb(ctx, "c_xt", [P, KD, N])
        xt3 = sb(ctx, "c_xt3", [P, KD, N])
        st1, mv1, rs1 = sb(ctx, "c_st1", [P, T, 6]), sb(ctx, "c_mv1", [P, T, 2]), sb(ctx, "c_rs1", [P, T])
        st3, mv3, rs3 = sb(ctx, "c_st3", [P, T, 6]), sb(ctx, "c_mv3", [P, T, 2]), sb(ctx, "c_rs3", [P, T])
        xp = sb(ctx, "c_xp", [P, T, D])
        xpt = sb(ctx, "c_xpt", [P, GRP, N])
        xct = sb(ctx, "c_xct", [P, HEADS, N])
        att = sb(ctx, "c_att", [P, 2, HG, N])
        ot = sb(ctx, "c_ot", [P, GRP, N])
        sh = sb(ctx, "c_sh", [P, KHS, N])
        hs = sb(ctx, "c_hs", [P, KHS, N])
        sg = sb(ctx, "c_sg", [P, T, E1])
        top = sb(ctx, "c_top", [P, T, 8])
        idx = sb(ctx, "c_idx", [P, T, 8], U32)
        idf = sb(ctx, "c_idf", [P, 2, T])
        oh = sb(ctx, "c_oh", [P, 2, T, E1])
        member = sb(ctx, "c_member", [P, T + 1, E1], BF16)
        pos = sb(ctx, "c_pos", [P, T, E1])
        own = sb(ctx, "c_own", [P, 2, T, E1])
        ownpos = sb(ctx, "c_ownpos", [P, 2, T])
        fits = sb(ctx, "c_fits", [P, 2, T])
        inside = sb(ctx, "c_inside", [P, 2, T])
        srow = sb(ctx, "c_srow", [P, 2, T])
        gsum = sb(ctx, "c_gsum", [P, 2, T])
        gk = sb(ctx, "c_gk", [P, 2, T])
        rows = sb(ctx, "c_rows", [P, 2, 2, T], U32)

        p_s = psum("p_s", [P, HG, N])
        p_o = psum("p_o", [P, GRP, N])
        p_w = psum("p_w", [P, 2, 512])
        p_w_tok = p_w[:].rearrange("p a (c d) -> p (a c) d", d=D)
        p_s_tok = p_s[:, 0:2, :].rearrange("p a (c d) -> p (a c) d", d=D)
        logit = p_w[:, 0, 0:T * E1].rearrange("p (t e) -> p t e", t=T)
        count = p_w[:, 1, 0:(T + 1) * E1].rearrange("p (t e) -> p t e", t=T + 1)

        s_w, s_in, init = sem("w"), [sem("in0"), sem("in1")], sem("init")
        grow_ready, gathered, x2_step = sem("grow"), sem("gathered"), sem("x2_step")
        ln1_step, ln1_rs, xn_ready = sem("ln1_step"), sem("ln1_rs"), sem("xn_ready")
        ln3_step, ln3_rs, xn3_ready = sem("ln3_step"), sem("ln3_rs"), sem("xn3_ready")
        tr_done, xt_ready, tr3_done, xt3_ready = sem("tr_done"), sem("xt_ready"), sem("tr3_done"), sem("xt3_ready")
        xp_done, xp_ready = sem("xp_done"), sem("xp_ready")
        xpt_done, xpt_ready = sem("xpt_done"), sem("xpt_ready")
        xct_done, xct_ready = sem("xct_done"), sem("xct_ready")
        s_done, prod_ready, att_ready, av_done = sem("s_done"), sem("prod_ready"), sem("att_ready"), sem("av_done")
        ot_ready, back_done, x3_ready = sem("ot_ready"), sem("back_done"), sem("x3_ready")
        log_done, sg_ready, sg_step = sem("log_done"), sem("sg_ready"), sem("sg_step")
        member_ready, count_done, rows_ready = sem("member"), sem("count_done"), sem("rows_ready")
        up_done, sh_ready, hs_ready = sem("up_done"), sem("sh_ready"), sem("hs_ready")
        down_done, x4_ready = sem("down_done"), sem("x4_ready")
        scattered = [sem("scattered0"), sem("scattered1")]
        UNITS = GRP * T
        NW = 8 + HEADS
        ROUTE_STEPS = 17

        block = ctx.enter_context(nc.Block())

        @block.sync
        def _(sp):
            sp.wait_ge(init, 1)
            for dst, name in ((wp[:], "wp"), (bpc[:], "bpc"), (wg[:], "wg"), (ws1[:], "ws1"),
                              (ws3[:], "ws3"), (ws2[:], "ws2")):
                sp.dma_start(dst, a[name]).then_inc(s_w, 16)
            sp.dma_start(bpr[:], a["bp"].partition_broadcast(P)).then_inc(s_w, 16)
            for i in range(HEADS):
                r = DH * (i % HG)
                sp.dma_start(cd[r:r + DH, i // HG, r:r + DH], a["ct"][i]).then_inc(s_w, 16)

            def graph(q, h, first, last):
                b = 2 * q + h
                if not (isinstance(q, int) and q == 0):
                    sp.wait_ge(prod_ready, 2 * UNITS * (b - 1))
                sp.dma_start(adj[:, h], a["adj"][b]).then_inc(s_in[h], 16)
            pairs(sp, B, graph)

        @block.gpsimd
        def _(pool):
            def gather(b):
                pool.wait_ge(grow_ready, b + 1)
                own_wait(pool, mark_pool)
                for i in range(2 * T):
                    pool.indirect_dma_start(
                        out=g[:, i, :], out_offset=None, in_=m["moe0_out"],
                        in_offset=bass.IndirectOffsetOnAxis(ap=grow[:, i:i + 1], axis=0)).then_inc(gathered, 16)

            def scale1(b):
                pool.wait_ge(ln1_step, 2 * b + 2)
                norm_scale(pool, mv1, m["half"], rs1, ln1_rs, 2 * b, mark_pool)

            def graph(q, h, first, last):
                b = 2 * q + h
                if not (last or (isinstance(q, int) and q == B // 2 - 1)):
                    gather(b + 2)
                if not last:
                    scale1(b + 1)
                pool.wait_ge(ln3_step, 2 * b + 2)
                norm_scale(pool, mv3, m["half"], rs3, ln3_rs, 2 * b, mark_pool)
                pool.wait_ge(rows_ready, b + 1)
                own_wait(pool, mark_pool)
                for k in range(2):
                    for t in range(T):
                        pool.indirect_dma_start(
                            out=m["moe1_in"], out_offset=bass.IndirectOffsetOnAxis(ap=rows[:, h, k, t:t + 1], axis=0),
                            in_=xn3[:, h, t, :], in_offset=None, bounds_check=E1 * CAP - 1, oob_is_err=False)\
                            .then_inc(scattered[h], 16)
            gather(0)
            gather(1)
            scale1(0)
            pairs(pool, B, graph)
            for h in range(2):
                pool.wait_ge(scattered[h], 16 * 2 * T * (B // 2))

        @block.tensor
        def _(pe):
            pe.wait_ge(s_w, 16 * (7 + HEADS))
            pe.wait_ge(init, 3)

            def project(b):
                pe.wait_ge(xn_ready, b + 1)
                transposes(pe, p_s[:, 0:2, :], xn, ident, tr_done)
                pe.wait_ge(xt_ready, b + 1)
                for t in range(T):
                    for k in range(KD):
                        mm = pe.matmul(p_s_tok[:, t, :], xt[:, k, t * P:(t + 1) * P], wp[:, k, :],
                                       start=(k == 0), stop=(k == KD - 1))
                    if t % 2:
                        mm.then_inc(xp_done, 1)
                for f in range(GRP):
                    for k in range(KD):
                        mm = pe.matmul(p_s[:, 2 + f, :], wp[:, k, f * P:(f + 1) * P], xt[:, k, :],
                                       start=(k == 0), stop=(k == KD - 1))
                    mm.then_inc(xpt_done, 1)

            def project_c(b):
                pe.wait_ge(xp_ready, TB * b + TB)
                for f in range(GRP):
                    pe.wait_ge(xpt_ready, GRP * b + f + 1)
                    pe.matmul(p_s[:, f, :], cd[:, f, :], xpt[:, f, :], start=True, stop=True).then_inc(xct_done, 1)

            def graph(q, h, first, last):
                b = 2 * q + h
                pe.wait_ge(xct_ready, HEADS * b + HEADS)

                def scores(u):
                    f, t = u // T, u % T
                    for i in range(HG):
                        if u > 0 and i % 2 == 0:
                            pe.wait_ge(prod_ready, 2 * (UNITS * b + u - 1) + i // 2 + 1)
                        mm = pe.matmul(p_s[:, i, :], xpt[:, f, t * P:(t + 1) * P], xct[:, HG * f + i, :],
                                       start=True, stop=True)
                        if i % 2:
                            mm.then_inc(s_done, 1)

                def values(u):
                    f, t = u // T, u % T
                    pe.wait_ge(att_ready, 2 * (UNITS * b + u) + 2)
                    for i in range(HG):
                        c = DH * (HG * f + i)
                        mm = pe.matmul(p_o[DH * i:DH * i + DH, f, :], xp[:, t, c:c + DH], att[:, u % 2, i, :],
                                       start=(t == 0), stop=(t == T - 1))
                    mm.then_inc(av_done, 1)

                scores(0)
                for u in range(1, UNITS):
                    scores(u)
                    values(u - 1)
                values(UNITS - 1)
                if not first:
                    pe.wait_ge(x4_ready, TB * b)
                for f in range(GRP):
                    pe.wait_ge(ot_ready, GRP * b + f + 1)
                    for t in range(T):
                        mm = pe.transpose(p_w_tok[:, t, f * P:(f + 1) * P], ot[:, f, t * P:(t + 1) * P], ident)
                mm.then_inc(back_done, 1)
                if not last:
                    project(b + 1)
                pe.wait_ge(xn3_ready, b + 1)
                transposes(pe, p_w, xn3[:, h], ident, tr3_done)
                if not last:
                    project_c(b + 1)
                pe.wait_ge(xt3_ready, b + 1)
                for t in range(T):
                    for k in range(KD):
                        mm = pe.matmul(logit[:, t, :], xt3[:, k, t * P:(t + 1) * P], wg[:, k, :],
                                       start=(k == 0), stop=(k == KD - 1))
                mm.then_inc(log_done, 1)
                for c in range(KHS):
                    for k in range(KD):
                        pe.matmul(p_s[:, 2 + c, :], ws1[:, k, c * P:(c + 1) * P], xt3[:, k, :],
                                  start=(k == 0), stop=(k == KD - 1))
                    for k in range(KD):
                        mm = pe.matmul(p_o[:, c, :], ws3[:, k, c * P:(c + 1) * P], xt3[:, k, :],
                                       start=(k == 0), stop=(k == KD - 1))
                    mm.then_inc(up_done, 1)
                pe.wait_ge(member_ready, b + 1)
                count_before(pe, m, count, member, count_done)
                pe.wait_ge(sg_step, ROUTE_STEPS * b + 8)
                for t in range(T):
                    for c in range(KHS):
                        if t == 0:
                            pe.wait_ge(hs_ready, KHS * b + c + 1)
                        mm = pe.matmul(p_w_tok[:, t, :], hs[:, c, t * P:(t + 1) * P], ws2[:, c, :],
                                       start=(c == 0), stop=(c == KHS - 1))
                    if t % 2:
                        mm.then_inc(down_done, 1)
            project(0)
            project_c(0)
            pairs(pe, B, graph)

        @block.scalar
        def _(act):
            act.wait_ge(s_w, 16 * (7 + HEADS))

            def evac_in(b):
                act.wait_ge(tr_done, b + 1)
                act.activation(xt[:], p_s[:, 0:2, :], ACT.Copy).then_inc(xt_ready, 1)
                for f in range(GRP):
                    act.wait_ge(xpt_done, GRP * b + f + 1)
                    act.activation(xpt[:, f, :], p_s[:, 2 + f, :], ACT.Identity, bias=bpc[:, f:f + 1])\
                       .then_inc(xpt_ready, 1)

            def evac_c(b, f):
                act.wait_ge(xct_done, GRP * b + f + 1)
                for i in range(HG):
                    r = slice(DH * i, DH * i + DH)
                    act.activation(xct[r, HG * f + i, :], p_s[r, f, :], ACT.Copy).then_inc(xct_ready, 1)

            def graph(q, h, first, last):
                b = 2 * q + h
                for u in range(UNITS):
                    for i in range(2):
                        n = 2 * (UNITS * b + u) + i + 1
                        act.wait_ge(prod_ready, n)
                        part = att[:, u % 2, 2 * i:2 * i + 2, :]
                        act.activation(part, part, ACT.Tanh).then_inc(att_ready, 1)
                act.wait_ge(av_done, UNITS * b + UNITS)
                for f in range(GRP):
                    act.activation(ot[:, f, :], p_o[:, f, :], ACT.Relu).then_inc(ot_ready, 1)
                if not last:
                    evac_in(b + 1)
                act.wait_ge(tr3_done, b + 1)
                act.activation(xt3[:], p_w[:], ACT.Copy).then_inc(xt3_ready, 1)
                if not last:
                    evac_c(b + 1, 0)
                act.wait_ge(log_done, b + 1)
                act.activation(sg[:], logit, ACT.Exp, scale=-1.0).then_inc(sg_ready, 1)
                for c in range(KHS):
                    act.wait_ge(up_done, KHS * b + c + 1)
                    act.activation(sh[:, c, :], p_s[:, 2 + c, :], ACT.Silu).then_inc(sh_ready, 1)
                if not last:
                    evac_c(b + 1, 1)
            evac_in(0)
            evac_c(0, 0)
            evac_c(0, 1)
            pairs(act, B, graph)

        @block.vector
        def _(dve):
            dve.memset(cd[:], 0.0).then_inc(init, 1)
            dve.memset(xct[:], 0.0).then_inc(init, 1)
            dve.memset(member[:], 0.0).then_inc(init, 1)
            dve.wait_ge(s_w, 16 * (7 + HEADS))

            def fetch(b):
                dve.tensor_copy(ggate[:], m["gate0"][:, bass.ds(b * 2 * T, 2 * T)])
                dve.tensor_copy(grow[:], m["rows0"][:, bass.ds(b * 2 * T, 2 * T)]).then_inc(grow_ready, 1)

            def add_moe0(b, fetch_next):
                dve.wait_ge(gathered, 16 * 2 * T * (b + 1))
                dve.wait_ge(grow_ready, b + 1)
                for k in range(2):
                    for t in range(T):
                        if k == 1:
                            dve.wait_ge(x2_step, 2 * T * b + t + 1)
                        dve.scalar_tensor_tensor(out=x[:, b * T + t, :], in0=g[:, k * T + t, :],
                                                 scalar=ggate[:, k * T + t:k * T + t + 1],
                                                 in1=x[:, b * T + t, :], op0=ALU.mult, op1=ALU.add)\
                           .then_inc(x2_step, 1)
                dve.wait_ge(x2_step, 2 * T * (b + 1))
                if fetch_next:
                    fetch(b + 1)

            def norm1_apply(b):
                dve.wait_ge(ln1_rs, 2 * b + 2)
                norm_apply(dve, x, b, mv1, rs1, xn, xn_ready)

            def evac_projection(b):
                for c in range(TB):
                    dve.wait_ge(xp_done, TB * b + c + 1)
                    dve.tensor_tensor(xp[:, 2 * c:2 * c + 2, :], p_s_tok[:, 2 * c:2 * c + 2, :],
                                      bpr[:].unsqueeze(1).broadcast_to([P, 2, D]), ALU.add).then_inc(xp_ready, 1)

            fetch(0)
            add_moe0(0, True)
            norm_stats(dve, x, 0, st1, mv1, ln1_step, 0, mark_dve)
            norm1_apply(0)
            evac_projection(0)

            def graph(q, h, first, last):
                b = 2 * q + h
                dve.wait_ge(s_in[h], 16 * (q + 1))
                for u in range(UNITS):
                    t = u % T
                    if u >= 2:
                        dve.wait_ge(av_done, UNITS * b + u - 1)
                    for i in range(2):
                        dve.wait_ge(s_done, 2 * (UNITS * b + u) + i + 1)
                        ins = dve.tensor_tensor(att[:, u % 2, 2 * i:2 * i + 2, :], p_s[:, 2 * i:2 * i + 2, :],
                                                adj[:, h, t, :].unsqueeze(1).broadcast_to([P, 2, N]), ALU.mult)
                        ins.then_inc(prod_ready, 1)
                    if u == 1 and not last:
                        add_moe0(b + 1, not (isinstance(q, int) and q == B // 2 - 1))
                    if u == 3 and not last:
                        norm_stats(dve, x, b + 1, st1, mv1, ln1_step, 2 * (b + 1), mark_dve)
                    if u == 5 and not last:
                        norm1_apply(b + 1)
                dve.wait_ge(back_done, b + 1)
                xb = x[:, bass.ds(b * T, T), :]
                dve.tensor_tensor(xb, xb, p_w_tok, ALU.add).then_inc(x3_ready, 1)
                dve.wait_ge(x3_ready, b + 1)
                if not (isinstance(q, int) and q == 0):
                    dve.wait_ge(scattered[h], 16 * 2 * T * q)
                norm_stats(dve, x, b, st3, mv3, ln3_step, 2 * b, mark_dve)
                dve.wait_ge(ln3_rs, 2 * b + 2)
                norm_apply(dve, x, b, mv3, rs3, xn3[:, h], xn3_ready)
                if not last:
                    evac_projection(b + 1)
                s = ROUTE_STEPS * b
                dve.wait_ge(sg_ready, b + 1)
                dve.tensor_scalar(sg[:], sg[:], 1.0, None, ALU.add).then_inc(sg_step, 1)
                dve.wait_ge(sg_step, s + 1)
                dve.reciprocal(sg[:], sg[:]).then_inc(sg_step, 1)
                dve.wait_ge(sg_step, s + 2)
                own_wait(dve, mark_dve)
                for t in range(T):
                    ins = dve.max(top[:, t, :], sg[:, t, :])
                ins.then_inc(sg_step, 1)
                dve.wait_ge(sg_step, s + 3)
                own_wait(dve, mark_dve)
                for t in range(T):
                    ins = dve.max_index(idx[:, t, :], top[:, t, :], sg[:, t, :])
                ins.then_inc(sg_step, 1)
                dve.wait_ge(sg_step, s + 4)
                dve.tensor_copy(idf[:], idx[:, :, 0:2].rearrange("p t k -> p k t")).then_inc(sg_step, 1)
                dve.wait_ge(sg_step, s + 5)
                iota = m["consts"][:, C_IOTA:C_IOTA + E1].unsqueeze(1).broadcast_to([P, T, E1])
                for k in range(2):
                    ins = dve.tensor_tensor(oh[:, k], iota, idf[:, k, :].unsqueeze(2).broadcast_to([P, T, E1]),
                                            ALU.is_equal)
                ins.then_inc(sg_step, 1)
                dve.wait_ge(sg_step, s + 6)
                dve.tensor_tensor(member[:, 0:T, :], oh[:, 0], oh[:, 1], ALU.add).then_inc(member_ready, 1)
                for c in range(KHS):
                    dve.wait_ge(sh_ready, KHS * b + c + 1)
                    dve.tensor_tensor(hs[:, c, :], sh[:, c, :], p_o[:, c, :], ALU.mult).then_inc(hs_ready, 1)
                dve.wait_ge(count_done, b + 1)
                dve.tensor_tensor(pos[:], count[:, 0:T, :], m["count1"][:].unsqueeze(1).broadcast_to([P, T, E1]),
                                  ALU.add).then_inc(sg_step, 1)
                dve.wait_ge(sg_step, s + 7)
                dve.tensor_tensor(m["count1"][:], m["count1"][:], count[:, T, :], ALU.add)
                for k in range(2):
                    ins = dve.tensor_tensor(own[:, k], oh[:, k], pos[:], ALU.mult)
                ins.then_inc(sg_step, 1)
                dve.wait_ge(sg_step, s + 8)
                dve.tensor_reduce(ownpos[:], own[:], AX, ALU.add).then_inc(sg_step, 1)
                dve.wait_ge(sg_step, s + 9)
                dve.tensor_scalar(fits[:], ownpos[:], float(CAP), None, ALU.is_lt).then_inc(sg_step, 1)
                dve.tensor_scalar(srow[:], ownpos[:], float(CAP), SKIP, ALU.is_ge, ALU.mult)
                dve.tensor_scalar(inside[:], ownpos[:], float(CAP - 1), None, ALU.min)
                dve.tensor_tensor(gsum[:, 0, :], top[:, :, 0], top[:, :, 1], ALU.add).then_inc(sg_step, 1)
                dve.wait_ge(sg_step, s + 11)
                dve.tensor_scalar(gsum[:, 1, :], gsum[:, 0, :], 1e-20, None, ALU.add).then_inc(sg_step, 1)
                dve.tensor_tensor(srow[:], srow[:], ownpos[:], ALU.add)
                dve.wait_ge(sg_step, s + 12)
                dve.reciprocal(gsum[:, 0, :], gsum[:, 1, :]).then_inc(sg_step, 1)
                dve.wait_ge(sg_step, s + 13)
                dve.tensor_tensor(gk[:], top[:, :, 0:2].rearrange("p t k -> p k t"),
                                  gsum[:, 0, :].unsqueeze(1).broadcast_to([P, 2, T]), ALU.mult).then_inc(sg_step, 1)
                dve.wait_ge(sg_step, s + 14)
                dve.scalar_tensor_tensor(out=gk[:], in0=gk[:], scalar=ROUTE_SCALE, in1=fits[:],
                                         op0=ALU.mult, op1=ALU.mult).then_inc(sg_step, 1)
                dve.scalar_tensor_tensor(out=rows[:, h], in0=idf[:], scalar=float(CAP), in1=srow[:],
                                         op0=ALU.mult, op1=ALU.add).then_inc(rows_ready, 1)
                dve.scalar_tensor_tensor(out=m["rows1"][:, bass.ds(b * 2 * T, 2 * T)].rearrange("p (k t) -> p k t", k=2),
                                         in0=idf[:], scalar=float(CAP), in1=inside[:],
                                         op0=ALU.mult, op1=ALU.add).then_inc(sg_step, 1)
                dve.wait_ge(sg_step, s + 16)
                dve.tensor_copy(m["gate1"][:, bass.ds(b * 2 * T, 2 * T)].rearrange("p (k t) -> p k t", k=2), gk[:])\
                   .then_inc(sg_step, 1)
                for c in range(TB):
                    dve.wait_ge(down_done, TB * b + c + 1)
                    xc = x[:, bass.ds(b * T + 2 * c, 2), :]
                    dve.tensor_tensor(xc, xc, p_w_tok[:, 2 * c:2 * c + 2, :], ALU.add).then_inc(x4_ready, 1)
            pairs(dve, B, graph)


def moe1_phase(nc, a, m, sb):
    ident = m["ident"]
    with ExitStack() as ctx:
        def sem(name):
            return ctx.enter_context(nc.semaphore("d_" + name))

        mark_dve, mark_pool, mark_sp = sem("mark_dve"), sem("mark_pool"), sem("mark_sp")

        def psum(name, shape):
            return ctx.enter_context(nc.psum_tensor("d_" + name, shape, F32))

        w = sb(ctx, "d_w", [P, 2, W_END1])
        xin = sb(ctx, "d_xin", [P, 2, T, D])
        xt = sb(ctx, "d_xt", [P, KD, CAP])
        gate = sb(ctx, "d_gate", [P, CAP])
        ht = sb(ctx, "d_ht", [P, 2, CAP])
        y = sb(ctx, "d_y", [P, 2, T, D])
        p_tr = psum("p_tr", [P, KD, CAP])
        p_h = psum("p_h", [P, 2, 2, CAP])
        p_y = psum("p_y", [P, T, D])
        s_rows, s_up = [sem("rows0"), sem("rows1")], [sem("up0"), sem("up1")]
        s_down = [sem("down0"), sem("down1")]
        s_out = [sem("out0"), sem("out1")]
        tr_done, xt_ready, up_done = sem("tr_done"), sem("xt_ready"), sem("up_done")
        gate_ready, ht_ready, y_done, y_ready = sem("gate_ready"), sem("ht_ready"), sem("y_done"), sem("y_ready")
        rows_in = m["moe1_in"].rearrange("(e p t) d -> e p (t d)", p=P, t=T)
        rows_out = m["moe1_out"].rearrange("(e p t) d -> e p (t d)", p=P, t=T)

        block = ctx.enter_context(nc.Block())

        @block.sync
        def _(sp):
            def load_rows(q, h):
                sp.dma_start(xin[:, h].rearrange("p t d -> p (t d)"), rows_in[2 * q + h]).then_inc(s_rows[h], 16)

            def load_up(q, h):
                sp.dma_start(w[:, h, 0:W2_1], a["moe1_w"][2 * q + h][:, 0:W2_1]).then_inc(s_up[h], 16)

            def load_down(q, h):
                sp.dma_start(w[:, h, W2_1:W_END1], a["moe1_w"][2 * q + h][:, W2_1:W_END1]).then_inc(s_down[h], 16)

            def store(q, h):
                e = 2 * q + h
                sp.wait_ge(y_ready, TB * e + TB)
                sp.dma_start(rows_out[e], y[:, h].rearrange("p t d -> p (t d)")).then_inc(s_out[h], 16)

            def one(q, h, first, last):
                e = 2 * q + h
                ahead = not (isinstance(q, int) and q == E1 // 2 - 1)
                if ahead:
                    sp.wait_ge(up_done, 2 * e + 2)
                    load_rows(q + 1, h)
                    load_up(q + 1, h)
                if not first:
                    store(q - 1 + h, 1 - h)
                    if not last:
                        load_down(q + h, 1 - h)
            for h in range(2):
                load_rows(0, h)
                load_up(0, h)
                load_down(0, h)
            pairs(sp, E1, one)
            store(E1 // 2 - 1, 1)
            for h in range(2):
                sp.wait_ge(s_out[h], 16 * (E1 // 2))

        @block.tensor
        def _(pe):
            def turn(q, h):
                pe.wait_ge(s_rows[h], 16 * (q + 1))
                transposes(pe, p_tr, xin[:, h], ident, tr_done)

            def down(q, h, first):
                e = 2 * q + h
                pe.wait_ge(s_down[h], 16 * (q + 1))
                pe.wait_ge(ht_ready, e + 1)
                for t in range(T):
                    if not first and t % 2 == 0:
                        pe.wait_ge(y_ready, TB * (e - 1) + t // 2 + 1)
                    mm = pe.matmul(p_y[:, t, :], ht[:, h, t * P:(t + 1) * P], w[:, h, W2_1:W2_1 + D],
                                   start=True, stop=True)
                    if t % 2:
                        mm.then_inc(y_done, 1)

            def one(q, h, first, last):
                e = 2 * q + h
                pe.wait_ge(s_up[h], 16 * (q + 1))
                pe.wait_ge(xt_ready, e + 1)
                for i, col in enumerate((W1_1, W3_1)):
                    for k in range(KD):
                        mm = pe.matmul(p_h[:, h, i, :], w[:, h, col + k * H1:col + (k + 1) * H1], xt[:, k, :],
                                       start=(k == 0), stop=(k == KD - 1))
                    mm.then_inc(up_done, 1)
                if not last:
                    turn(q + h, 1 - h)
                if not first:
                    down(q - 1 + h, 1 - h, h == 1 and isinstance(q, int) and q == 0)
            turn(0, 0)
            pairs(pe, E1, one)
            down(E1 // 2 - 1, 1, False)

        @block.scalar
        def _(act):
            def evac(e):
                act.wait_ge(tr_done, e + 1)
                act.activation(xt[:], p_tr[:], ACT.Copy).then_inc(xt_ready, 1)

            def one(q, h, first, last):
                e = 2 * q + h
                act.wait_ge(up_done, 2 * e + 1)
                if not first:
                    act.wait_ge(ht_ready, e)
                act.activation(gate[:], p_h[:, h, 0, :], ACT.Silu).then_inc(gate_ready, 1)
                if not last:
                    evac(e + 1)
            evac(0)
            pairs(act, E1, one)

        @block.vector
        def _(dve):
            def results(q, h):
                e = 2 * q + h
                if not (isinstance(q, int) and q == 0):
                    dve.wait_ge(s_out[h], 16 * q)
                for c in range(TB):
                    dve.wait_ge(y_done, TB * e + c + 1)
                    dve.tensor_copy(y[:, h, 2 * c:2 * c + 2, :], p_y[:, 2 * c:2 * c + 2, :]).then_inc(y_ready, 1)

            def one(q, h, first, last):
                e = 2 * q + h
                dve.wait_ge(gate_ready, e + 1)
                dve.wait_ge(up_done, 2 * e + 2)
                dve.tensor_tensor(ht[:, h, :], gate[:], p_h[:, h, 1, :], ALU.mult).then_inc(ht_ready, 1)
                if not first:
                    results(q - 1 + h, 1 - h)
            pairs(dve, E1, one)
            results(E1 // 2 - 1, 1)


def combine_phase(nc, a, m, sb, out):
    x = m["x"]
    with ExitStack() as ctx:
        def sem(name):
            return ctx.enter_context(nc.semaphore("e_" + name))

        mark_dve, mark_pool, mark_sp = sem("mark_dve"), sem("mark_pool"), sem("mark_sp")

        g = sb(ctx, "e_g", [P, 2, 2 * T, D])
        grow = sb(ctx, "e_grow", [P, 2, 2 * T], U32)
        ggate = sb(ctx, "e_ggate", [P, 2, 2 * T])
        grow_ready, step, s_out = sem("grow"), sem("step"), sem("out")
        gathered = [sem("gathered0"), sem("gathered1")]
        block = ctx.enter_context(nc.Block())

        @block.gpsimd
        def _(pool):
            def graph(q, h, first, last):
                b = 2 * q + h
                pool.wait_ge(grow_ready, b + 1)
                own_wait(pool, mark_pool)
                for i in range(2 * T):
                    pool.indirect_dma_start(
                        out=g[:, h, i, :], out_offset=None, in_=m["moe1_out"],
                        in_offset=bass.IndirectOffsetOnAxis(ap=grow[:, h, i:i + 1], axis=0)).then_inc(gathered[h], 16)
            pairs(pool, B, graph)

        @block.vector
        def _(dve):
            def fetch(q, h):
                b = 2 * q + h
                dve.tensor_copy(ggate[:, h, :], m["gate1"][:, bass.ds(b * 2 * T, 2 * T)])
                dve.tensor_copy(grow[:, h, :], m["rows1"][:, bass.ds(b * 2 * T, 2 * T)]).then_inc(grow_ready, 1)

            fetch(0, 0)

            def graph(q, h, first, last):
                b = 2 * q + h
                if not last:
                    fetch(q + h, 1 - h)
                dve.wait_ge(grow_ready, b + 1)
                dve.wait_ge(gathered[h], 16 * 2 * T * (q + 1))
                for k in range(2):
                    for t in range(T):
                        if k == 1:
                            dve.wait_ge(step, 2 * T * b + t + 1)
                        dve.scalar_tensor_tensor(out=x[:, b * T + t, :], in0=g[:, h, k * T + t, :],
                                                 scalar=ggate[:, h, k * T + t:k * T + t + 1],
                                                 in1=x[:, b * T + t, :], op0=ALU.mult, op1=ALU.add)\
                           .then_inc(step, 1)
                dve.wait_ge(step, 2 * T * (b + 1))
            pairs(dve, B, graph)

        @block.sync
        def _(sp):
            def graph(q, h, first, last):
                b = 2 * q + h
                sp.wait_ge(step, 2 * T * (b + 1))
                sp.dma_start(out[:, bass.ds(b * T, T), :], x[:, bass.ds(b * T, T), :]).then_inc(s_out, 16)
            pairs(sp, B, graph)
            sp.wait_ge(s_out, 16 * B)


def by_rows(w, k):
    return np.ascontiguousarray(w.reshape(k, P, -1).transpose(1, 0, 2))


def kernel(x, adj, L0_gnn_W1, L0_gnn_b1, L0_gnn_W2, L0_gnn_b2, L0_gnn_W3, L0_gnn_b3, L0_ffn_Wr, L0_ffn_br,
           L0_ffn_W1, L0_ffn_b1, L0_ffn_W2, L0_ffn_b2, L1_gnn_Wp, L1_gnn_bp, L1_gnn_C, L1_ffn_gate_w,
           L1_ffn_w1, L1_ffn_w3, L1_ffn_w2, L1_ffn_sw1, L1_ffn_sw3, L1_ffn_sw2):
    import concourse.bacc as bacc
    from concourse.bass_utils import run_bass_kernel_spmd

    flat = lambda w: w.reshape(w.shape[0], P, -1)
    consts = np.zeros((P, C_END), np.float32)
    consts[:, C_ID:C_ID + P] = np.eye(P)
    consts[:, C_TRI:C_TRI + P] = np.triu(np.ones((P, P)), 1)
    consts[:, C_ONE:C_ONE + P] = 1
    consts[:, C_IOTA:C_IOTA + E1] = np.arange(E1)
    consts[:, C_THR:C_THR + NTHR] = np.arange(NTHR) * BLK
    consts[:, C_BLK:C_BLK + NBLK] = np.arange(NBLK)
    rows = lambda w, k: w.reshape(w.shape[0], k, P, -1).transpose(0, 2, 1, 3).reshape(w.shape[0], P, -1)
    ins = {
        "consts": consts,
        "x": x.reshape(B * T, P, D).transpose(1, 0, 2),
        "adj": adj.transpose(0, 2, 1).reshape(B, T, P, N).transpose(0, 2, 1, 3),
        "w1": by_rows(L0_gnn_W1, KD), "w2": by_rows(L0_gnn_W2, KD), "w3": by_rows(L0_gnn_W3, KD),
        "b1": L0_gnn_b1.reshape(KD, P).T, "b2": L0_gnn_b2.reshape(KD, P).T, "b3": L0_gnn_b3,
        "wr": by_rows(L0_ffn_Wr.T, KD), "br": L0_ffn_br,
        "moe0_w": np.concatenate([rows(L0_ffn_W1, KD), rows(L0_ffn_W2, KH0),
                                  L0_ffn_b1.reshape(E0, KH0, P).transpose(0, 2, 1)], axis=2),
        "moe0_b2": L0_ffn_b2,
        "wp": by_rows(L1_gnn_Wp.transpose(1, 0, 2).reshape(D, HEADS * DH), KD),
        "bp": L1_gnn_bp.reshape(HEADS * DH), "bpc": L1_gnn_bp.reshape(GRP, P).T,
        "ct": L1_gnn_C.transpose(0, 2, 1),
        "wg": by_rows(L1_ffn_gate_w.T, KD),
        "ws1": by_rows(L1_ffn_sw1, KD), "ws3": by_rows(L1_ffn_sw3, KD), "ws2": by_rows(L1_ffn_sw2, KHS),
        "moe1_w": np.concatenate([rows(L1_ffn_w1, KD), rows(L1_ffn_w3, KD), L1_ffn_w2], axis=2),
    }
    ins = {k: np.ascontiguousarray(v) for k, v in ins.items()}
    nc = bacc.Bacc("TRN2", target_bir_lowering=False, num_devices=1)
    a = {k: nc.dram_tensor(f"in_{k}", v.shape, mybir.dt.from_np(v.dtype), kind="ExternalInput").ap()
         for k, v in ins.items()}
    out = nc.dram_tensor("out_x", (P, B * T, D), F32, kind="ExternalOutput").ap()
    build(nc, a, out)
    r = run_bass_kernel_spmd(nc, [{f"in_{k}": v for k, v in ins.items()}], core_ids=[0])
    return np.ascontiguousarray(r.results[0]["out_x"].transpose(1, 0, 2)).reshape(B, N, D)
```

```python
from contextlib import ExitStack

import numpy as np

import concourse.bass as bass
from concourse import mybir

F32 = mybir.dt.float32
F32R = mybir.dt.float32r
BF16 = mybir.dt.bfloat16
I32 = mybir.dt.int32
U32 = mybir.dt.uint32
ALU = mybir.AluOpType
ACT = mybir.ActivationFunctionType
AX = mybir.AxisListType.X

P = 128
B, N, D = 16, 512, 256
T = N // P
TB = T // 2
KD = D // P
TOK = B * N

E0, H0 = 8, 512
KH0 = H0 // P
BLK = 512
REGION = TOK + BLK
SPARE = E0 * REGION
NBLK = 2 * TOK // BLK + E0
NTHR = TOK // BLK
PAIRS = 2 * TOK // P

HEADS, DH = 8, 32
GRP = 2
HG = HEADS // GRP

E1, H1, CAP = 64, 128, 512
HS = 256
KHS = HS // P
ROUTE_SCALE = 2.5
SKIP = float(1 << 20)

EPS = 1e-5

C_ID, C_TRI, C_ONE, C_IOTA, C_THR, C_BLK, C_END = np.cumsum([0, P, P, P, E1, NTHR, NBLK])
W1_1, W3_1, W2_1, W_END1 = np.cumsum([0, KD * H1, KD * H1, D])


def pairs(eng, n, body):
    body(0, 0, True, False)
    body(0, 1, False, n == 2)
    if n > 4:
        with eng.Fori(1, n // 2 - 1) as q:
            body(q, 0, False, False)
            body(q, 1, False, False)
    if n > 2:
        body(n // 2 - 1, 0, False, False)
        body(n // 2 - 1, 1, False, True)


def build(nc, a, out):
    with ExitStack() as whole:
        def sb(ctx, name, shape, dt=F32):
            return ctx.enter_context(nc.sbuf_tensor(name, shape, dt))

        x = sb(whole, "x", [P, B * T, D])
        consts = sb(whole, "consts", [P, C_END])
        tri = sb(whole, "tri", [P, P], BF16)
        ones = sb(whole, "ones", [P, P], BF16)
        half = sb(whole, "half", [P, T])
        adj = sb(whole, "adj", [P, 2, T, N])
        slot0 = sb(whole, "slot0", [P, PAIRS])
        rows0 = sb(whole, "rows0", [P, PAIRS], U32)
        gate0 = sb(whole, "gate0", [P, PAIRS])
        rows1 = sb(whole, "rows1", [P, PAIRS], U32)
        gate1 = sb(whole, "gate1", [P, PAIRS])
        count0 = sb(whole, "count0", [P, E0])
        count1 = sb(whole, "count1", [P, E1])
        ident = consts[:, C_ID:C_ID + P]

        moe0_in = nc.dram_tensor("moe0_in", [SPARE + BLK, D], F32).ap()
        moe0_out = nc.dram_tensor("moe0_out", [NBLK * BLK, D], F32).ap()
        moe1_in = nc.dram_tensor("moe1_in", [E1 * CAP, D], F32).ap()
        moe1_out = nc.dram_tensor("moe1_out", [E1 * CAP, D], F32).ap()

        m = dict(x=x, consts=consts, tri=tri, ones=ones, half=half, adj=adj, rows0=rows0,
                 gate0=gate0, rows1=rows1, gate1=gate1, count0=count0, count1=count1, ident=ident, slot0=slot0,
                 moe0_in=moe0_in, moe0_out=moe0_out, moe1_in=moe1_in, moe1_out=moe1_out)
        gcn_phase(nc, a, m, sb)
        moe0_phase(nc, a, m, sb)
        attention_phase(nc, a, m, sb)
        moe1_phase(nc, a, m, sb)
        combine_phase(nc, a, m, sb, out)


def own_wait(eng, mark):
    eng.sem_inc(mark, 1)


def exact(pe, out, lhs, rhs, start, stop):
    (lh, ll), (rh, rl) = lhs, rhs
    pe.matmul(out, lh, rh, start=start, stop=False)
    pe.matmul(out, lh, rl, start=False, stop=False)
    return pe.matmul(out, ll, rh, start=False, stop=stop)


def low_part(dve, low, whole, high):
    return dve.tensor_tensor(low, whole, high.bitcast(F32), ALU.subtract)


def transposes(pe, dst, src, ident, ready):
    for k in range(KD):
        for t in range(T):
            mm = pe.transpose(dst[:, k, t * P:(t + 1) * P], src[:, t, k * P:(k + 1) * P], ident)
    mm.then_inc(ready, 1)


def norm_stats(dve, x, b, stats, mv, step, at, mark):
    own_wait(dve, mark)
    for t in range(T):
        ins = dve.bn_stats(stats[:, t, :], x[:, b * T + t, :])
    ins.then_inc(step, 1)
    dve.wait_ge(step, at + 1)
    own_wait(dve, mark)
    for t in range(T):
        ins = dve.bn_aggr(mv[:, t, :], stats[:, t, :])
    ins.then_inc(step, 1)


def norm_scale(pool, mv, half, rstd, step, at, mark):
    own_wait(pool, mark)
    pool.tensor_scalar(rstd[:], mv[:, :, 1], EPS, None, ALU.add).then_inc(step, 1)
    pool.wait_ge(step, at + 1)
    pool.tensor_tensor(rstd[:], rstd[:], half[:], ALU.pow).then_inc(step, 1)


def norm_apply(dve, x, b, mv, rstd, xn, ready):
    for t in range(T):
        ins = dve.tensor_scalar(xn[:, t, :], x[:, b * T + t, :], mv[:, t, 0:1], rstd[:, t:t + 1],
                                ALU.subtract, ALU.mult)
    ins.then_inc(ready, 1)


def gcn_phase(nc, a, m, sb):
    x, adj, ident = m["x"], m["adj"], m["ident"]
    with ExitStack() as ctx:
        def sem(name):
            return ctx.enter_context(nc.semaphore("a_" + name))

        mark_dve, mark_pool, mark_sp = sem("mark_dve"), sem("mark_pool"), sem("mark_sp")

        def psum(name, shape):
            return ctx.enter_context(nc.psum_tensor("a_" + name, shape, F32))

        w = sb(ctx, "a_w", [P, 3, KD, D])
        zeros = sb(ctx, "a_zeros", [P, T * D])
        bias = sb(ctx, "a_bias", [P, 2, KD])
        bias3 = sb(ctx, "a_bias3", [P, D])
        wr = sb(ctx, "a_wr", [P, KD, E0])
        br = sb(ctx, "a_br", [P, E0])
        wh, wl = sb(ctx, "a_wh", [P, 3, KD, D], F32R), sb(ctx, "a_wl", [P, 3, KD, D], F32R)
        adjh, adjl = sb(ctx, "a_adjh", [P, 2, T, N], F32R), sb(ctx, "a_adjl", [P, 2, T, N], F32R)
        feat = sb(ctx, "a_feat", [P, KD, N])
        fh, fl = sb(ctx, "a_fh", [P, KD, N], F32R), sb(ctx, "a_fl", [P, KD, N], F32R)
        suph, supl = sb(ctx, "a_suph", [P, T, D], F32R), sb(ctx, "a_supl", [P, T, D], F32R)
        xn1 = sb(ctx, "a_xn1", [P, T, D])
        xn2 = sb(ctx, "a_xn2", [P, 2, T, D])
        xt2 = sb(ctx, "a_xt2", [P, KD, N])
        st1, mv1, rs1 = sb(ctx, "a_st1", [P, T, 6]), sb(ctx, "a_mv1", [P, T, 2]), sb(ctx, "a_rs1", [P, T])
        st2, mv2, rs2 = sb(ctx, "a_st2", [P, T, 6]), sb(ctx, "a_mv2", [P, T, 2]), sb(ctx, "a_rs2", [P, T])
        lg = sb(ctx, "a_lg", [P, T, E0])
        mx = sb(ctx, "a_mx", [P, T])
        ex = sb(ctx, "a_ex", [P, T, E0])
        sm = sb(ctx, "a_sm", [P, 2, T])
        pr = sb(ctx, "a_pr", [P, T, E0])
        top = sb(ctx, "a_top", [P, T, 8])
        idx = sb(ctx, "a_idx", [P, T, 8], U32)
        idf = sb(ctx, "a_idf", [P, 2, T])
        oh = sb(ctx, "a_oh", [P, 2, T, E0])
        member = sb(ctx, "a_member", [P, T + 1, E0], BF16)
        pos = sb(ctx, "a_pos", [P, T, E0])
        own = sb(ctx, "a_own", [P, 2, T, E0])
        ownpos = sb(ctx, "a_ownpos", [P, 2, T])
        rows = sb(ctx, "a_rows", [P, 2, 2, T], U32)

        p_agg = psum("p_agg", [P, 2, 512])
        p_sup = psum("p_sup", [P, T, D])
        p_tr = psum("p_tr", [P, KD, N])
        p_log = psum("p_log", [P, 512])
        p_pos = psum("p_pos", [P, 512])
        logit = p_log[:, 0:T * E0].rearrange("p (t e) -> p t e", t=T)
        count = p_pos[:, 0:(T + 1) * E0].rearrange("p (t e) -> p t e", t=T + 1)

        s_const, s_w, s_in = sem("const"), sem("w"), [sem("in0"), sem("in1")]
        s_x = [sem("x0"), sem("x1")]
        init_dve, init_pool = sem("init_dve"), sem("init_pool")
        ln1_step, ln1_rs, xn1_ready = sem("ln1_step"), sem("ln1_rs"), sem("xn1_ready")
        ln2_step, ln2_rs, xn2_ready = sem("ln2_step"), sem("ln2_rs"), sem("xn2_ready")
        tr1_done, in_hi, in_lo = sem("tr1_done"), sem("in_hi"), sem("in_lo")
        w_hi, w_lo, adj_hi, adj_lo = sem("w_hi"), sem("w_lo"), sem("adj_hi"), sem("adj_lo")
        tr2_done, xt2_ready = sem("tr2_done"), sem("xt2_ready")
        sup_done, sup_hi, sup_lo = sem("sup_done"), sem("sup_hi"), sem("sup_lo")
        agg_done, feat_hi, feat_ready, feat_lo = sem("agg_done"), sem("feat_hi"), sem("feat_ready"), sem("feat_lo")
        biased, x1_ready = sem("biased"), sem("x1_ready")
        log_done, lg_ready, ex_ready = sem("log_done"), sem("lg_ready"), sem("ex_ready")
        route_step, member_ready, count_done = sem("route_step"), sem("member_ready"), sem("count_done")
        rows_ready = sem("rows_ready")
        scattered = [sem("scattered0"), sem("scattered1")]
        s_zero = sem("zero")
        ROUTE_STEPS = 12

        block = ctx.enter_context(nc.Block())

        @block.sync
        def _(sp):
            def load_x(b, h):
                sp.dma_start(x[:, bass.ds(b * T, T), :], a["x"][:, bass.ds(b * T, T), :]).then_inc(s_x[h], 16)
            load_x(0, 0)
            sp.dma_start(m["consts"][:], a["consts"]).then_inc(s_const, 16)
            for dst, name in ((w[:, 0], "w1"), (w[:, 1], "w2"), (w[:, 2], "w3"), (bias[:, 0, :], "b1"),
                              (bias[:, 1, :], "b2"), (wr[:], "wr")):
                sp.dma_start(dst, a[name]).then_inc(s_w, 16)
            sp.dma_start(bias3[:], a["b3"].partition_broadcast(P)).then_inc(s_w, 16)
            sp.dma_start(br[:], a["br"].partition_broadcast(P)).then_inc(s_w, 16)
            sp.wait_ge(init_pool, 2)
            zero_rows = m["moe1_in"].rearrange("(i p t) d -> i p (t d)", p=P, t=T)
            def graph(q, h, first, last):
                b = 2 * q + h
                if not (first or (h == 1 and isinstance(q, int) and q == 0)):
                    sp.wait_ge(adj_lo, 2 * (b - 1))
                sp.dma_start(adj[:, h], a["adj"][b]).then_inc(s_in[h], 16)
                if not first:
                    load_x(b, h)
                for i in range(E1 // B):
                    sp.dma_start(zero_rows[b * (E1 // B) + i], zeros[:]).then_inc(s_zero, 16)
            pairs(sp, B, graph)
            sp.dma_start(m["moe0_in"][SPARE:SPARE + BLK, :].rearrange("(p t) d -> p (t d)", p=P),
                         zeros[:]).then_inc(s_zero, 16)
            sp.wait_ge(s_zero, 16 * (E1 + 1))

        @block.gpsimd
        def _(pool):
            pool.memset(m["half"][:], -0.5).then_inc(init_pool, 1)
            pool.memset(zeros[:], 0.0).then_inc(init_pool, 1)
            pool.wait_ge(init_pool, 2)

            def scale1(b):
                pool.wait_ge(ln1_step, 2 * b + 2)
                norm_scale(pool, mv1, m["half"], rs1, ln1_rs, 2 * b, mark_pool)

            def scatter(q, h):
                b = 2 * q + h
                pool.wait_ge(rows_ready, b + 1)
                own_wait(pool, mark_pool)
                for k in range(2):
                    for t in range(T):
                        pool.indirect_dma_start(
                            out=m["moe0_in"], out_offset=bass.IndirectOffsetOnAxis(ap=rows[:, h, k, t:t + 1], axis=0),
                            in_=xn2[:, h, t, :], in_offset=None).then_inc(scattered[h], 16)

            def graph(q, h, first, last):
                b = 2 * q + h
                if not last:
                    scale1(b + 1)
                pool.wait_ge(xn1_ready, b + 1)
                if first:
                    pool.wait_ge(s_w, 16 * 8)
                for t in range(T):
                    ins = pool.tensor_tensor(x[:, b * T + t, :], x[:, b * T + t, :], bias3[:], ALU.add)
                ins.then_inc(biased, 1)
                pool.wait_ge(ln2_step, 2 * b + 2)
                norm_scale(pool, mv2, m["half"], rs2, ln2_rs, 2 * b, mark_pool)
                if not first:
                    scatter(q - 1 + h, 1 - h)

            scale1(0)
            pairs(pool, B, graph)
            scatter(B // 2 - 1, 1)
            for h in range(2):
                pool.wait_ge(scattered[h], 16 * 2 * T * (B // 2))

        @block.tensor
        def _(pe):
            def transpose_in(b, h):
                pe.wait_ge(xn1_ready, b + 1)
                transposes(pe, p_tr, xn1, ident, tr1_done)

            def support(b, layer):
                hi, lo, n = (in_hi, in_lo, b + 1) if layer == 0 else (feat_hi, feat_lo, 4 * b + 2 * layer)
                pe.wait_ge(hi, n)
                for t in range(T):
                    tok = slice(t * P, (t + 1) * P)
                    for k in range(KD):
                        pe.matmul(p_sup[:, t, :], fh[:, k, tok], wh[:, layer, k, :], start=(k == 0), stop=False)
                        pe.matmul(p_sup[:, t, :], fh[:, k, tok], wl[:, layer, k, :], start=False, stop=False)
                    if t == 0:
                        pe.wait_ge(lo, n)
                    for k in range(KD):
                        mm = pe.matmul(p_sup[:, t, :], fl[:, k, tok], wh[:, layer, k, :],
                                       start=False, stop=(k == KD - 1))
                    if t % 2:
                        mm.then_inc(sup_done, 1)

            def aggregate(b, layer, h):
                s = 3 * TB * b + TB * layer
                for f in range(KD):
                    col = slice(f * P, (f + 1) * P)
                    for t in range(T):
                        if f == 0 and t % 2 == 0:
                            pe.wait_ge(sup_hi, s + t // 2 + 1)
                        pe.matmul(p_agg[:, f, :], suph[:, t, col], adjh[:, h, t, :], start=(t == 0), stop=False)
                        pe.matmul(p_agg[:, f, :], suph[:, t, col], adjl[:, h, t, :], start=False, stop=False)
                    for t in range(T):
                        if f == 0 and t % 2 == 0:
                            pe.wait_ge(sup_lo, s + t // 2 + 1)
                        mm = pe.matmul(p_agg[:, f, :], supl[:, t, col], adjh[:, h, t, :],
                                       start=False, stop=(t == T - 1))
                    mm.then_inc(agg_done, 1)

            def aggregate_out(b, h):
                out = p_agg[:].rearrange("p a (c d) -> p (a c) d", d=D)
                pe.wait_ge(sup_lo, 3 * TB * b + 3 * TB)
                for n in range(T):
                    tok = slice(n * P, (n + 1) * P)
                    for t in range(T):
                        mm = exact(pe, out[:, n, :], (adjh[:, h, t, tok], adjl[:, h, t, tok]),
                                   (suph[:, t, :], supl[:, t, :]), t == 0, t == T - 1)
                    if n % 2:
                        mm.then_inc(agg_done, 1)

            def route_logits(b):
                pe.wait_ge(xt2_ready, b + 1)
                for t in range(T):
                    for k in range(KD):
                        mm = pe.matmul(logit[:, t, :], xt2[:, k, t * P:(t + 1) * P], wr[:, k, :],
                                       start=(k == 0), stop=(k == KD - 1))
                mm.then_inc(log_done, 1)

            def route_counts(b):
                pe.wait_ge(member_ready, b + 1)
                count_before(pe, m, count, member, count_done)

            def graph(q, h, first, last):
                b = 2 * q + h
                support(b, 0)
                pe.wait_ge(adj_lo, 2 * b + 2)
                if not first:
                    pe.wait_ge(x1_ready, TB * b)
                aggregate(b, 0, h)
                if not first:
                    pe.wait_ge(xn2_ready, b)
                    transposes(pe, p_tr, xn2[:, 1 - h], ident, tr2_done)
                support(b, 1)
                if not first:
                    route_logits(b - 1)
                aggregate(b, 1, h)
                support(b, 2)
                if not last:
                    transpose_in(b + 1, 1 - h)
                aggregate_out(b, h)
                if not first:
                    route_counts(b - 1)

            pe.wait_ge(s_const, 16)
            pe.wait_ge(s_w, 16 * 8)
            pe.wait_ge(init_dve, 4)
            pe.wait_ge(w_lo, 1)
            transpose_in(0, 0)
            pairs(pe, B, graph)
            pe.wait_ge(xn2_ready, B)
            transposes(pe, p_tr, xn2[:, 1], ident, tr2_done)
            route_logits(B - 1)
            route_counts(B - 1)

        @block.scalar
        def _(act):
            def evac_in(b):
                act.wait_ge(tr1_done, b + 1)
                act.activation(fh[:], p_tr[:], ACT.Copy).then_inc(in_hi, 1)

            def split_adj(q, h, part):
                if part == 0:
                    act.wait_ge(s_in[h], 16 * (q + 1))
                rows = slice(part * TB, (part + 1) * TB)
                act.activation(adjh[:, h, rows, :], adj[:, h, rows, :], ACT.Copy).then_inc(adj_hi, 1)

            def evac_support(b, layer):
                for c in range(TB):
                    act.wait_ge(sup_done, 3 * TB * b + TB * layer + c + 1)
                    act.activation(suph[:, 2 * c:2 * c + 2, :], p_sup[:, 2 * c:2 * c + 2, :], ACT.Copy)\
                       .then_inc(sup_hi, 1)

            def evac_layer(b, layer):
                for f in range(KD):
                    act.wait_ge(agg_done, 6 * b + 2 * layer + f + 1)
                    act.activation(fh[:, f, :], p_agg[:, f, :], ACT.Relu, bias=bias[:, layer, f:f + 1])\
                       .then_inc(feat_hi, 1)
                    act.activation(feat[:, f, :], p_agg[:, f, :], ACT.Relu, bias=bias[:, layer, f:f + 1])\
                       .then_inc(feat_ready, 1)

            def evac_router(b):
                act.wait_ge(tr2_done, b + 1)
                act.activation(xt2[:], p_tr[:], ACT.Copy).then_inc(xt2_ready, 1)

            def exps(b):
                act.wait_ge(lg_ready, b + 1)
                act.activation(ex[:], lg[:], ACT.Exp).then_inc(ex_ready, 1)

            def graph(q, h, first, last):
                b = 2 * q + h
                evac_support(b, 0)
                if not last:
                    split_adj(q + h, 1 - h, 0)
                evac_layer(b, 0)
                if not first:
                    evac_router(b - 1)
                evac_support(b, 1)
                if not last:
                    split_adj(q + h, 1 - h, 1)
                evac_layer(b, 1)
                evac_support(b, 2)
                if not last:
                    evac_in(b + 1)
                if not first:
                    exps(b - 1)

            act.wait_ge(s_w, 16 * 8)
            act.activation(wh[:], w[:], ACT.Copy).then_inc(w_hi, 1)
            split_adj(0, 0, 0)
            split_adj(0, 0, 1)
            evac_in(0)
            pairs(act, B, graph)
            evac_router(B - 1)
            exps(B - 1)

        @block.vector
        def _(dve):
            dve.wait_ge(s_const, 16)
            dve.tensor_copy(m["tri"][:], m["consts"][:, C_TRI:C_TRI + P]).then_inc(init_dve, 1)
            dve.tensor_copy(m["ones"][:], m["consts"][:, C_ONE:C_ONE + P]).then_inc(init_dve, 1)
            dve.memset(member[:], 0.0).then_inc(init_dve, 1)
            dve.memset(m["count0"][:], 0.0)
            dve.memset(m["count1"][:], 0.0).then_inc(init_dve, 1)
            dve.wait_ge(init_dve, 4)
            dve.wait_ge(s_w, 16 * 8)

            def norm1_stats(q, h):
                b = 2 * q + h
                dve.wait_ge(s_x[h], 16 * (q + 1))
                norm_stats(dve, x, b, st1, mv1, ln1_step, 2 * b, mark_dve)

            def norm1_apply(b):
                dve.wait_ge(ln1_rs, 2 * b + 2)
                if not (isinstance(b, int) and b == 0):
                    dve.wait_ge(tr1_done, b)
                norm_apply(dve, x, b, mv1, rs1, xn1, xn1_ready)

            def split_in(b):
                dve.wait_ge(in_hi, b + 1)
                low_part(dve, fl[:], p_tr[:], fh[:]).then_inc(in_lo, 1)

            def split_adj(b, h, part):
                dve.wait_ge(adj_hi, 2 * b + part + 1)
                rows = slice(part * TB, (part + 1) * TB)
                low_part(dve, adjl[:, h, rows, :], adj[:, h, rows, :], adjh[:, h, rows, :]).then_inc(adj_lo, 1)

            def split_support(b, layer):
                for c in range(TB):
                    dve.wait_ge(sup_hi, 3 * TB * b + TB * layer + c + 1)
                    two = slice(2 * c, 2 * c + 2)
                    low_part(dve, supl[:, two, :], p_sup[:, two, :], suph[:, two, :]).then_inc(sup_lo, 1)

            def split_layer(b, layer):
                for f in range(KD):
                    dve.wait_ge(feat_ready, 4 * b + 2 * layer + f + 1)
                    low_part(dve, fl[:, f, :], feat[:, f, :], fh[:, f, :]).then_inc(feat_lo, 1)

            def residual_stats(q, h):
                b = 2 * q + h
                out = p_agg[:].rearrange("p a (c d) -> p (a c) d", d=D)
                dve.wait_ge(biased, b + 1)
                for c in range(TB):
                    dve.wait_ge(agg_done, 6 * b + 4 + c + 1)
                    xc = x[:, bass.ds(b * T + 2 * c, 2), :]
                    dve.tensor_tensor(xc, xc, out[:, 2 * c:2 * c + 2, :], ALU.add).then_inc(x1_ready, 1)
                dve.wait_ge(x1_ready, TB * b + TB)
                norm_stats(dve, x, b, st2, mv2, ln2_step, 2 * b, mark_dve)

            def norm2_apply(q, h):
                b = 2 * q + h
                dve.wait_ge(ln2_rs, 2 * b + 2)
                if not (isinstance(q, int) and q == 0):
                    dve.wait_ge(scattered[h], 16 * 2 * T * q)
                norm_apply(dve, x, b, mv2, rs2, xn2[:, h], xn2_ready)

            def route_choose(b):
                s = ROUTE_STEPS * b
                dve.wait_ge(log_done, b + 1)
                dve.tensor_tensor(lg[:], logit, br[:].unsqueeze(1).broadcast_to([P, T, E0]), ALU.add)\
                   .then_inc(route_step, 1)
                dve.wait_ge(route_step, s + 1)
                dve.tensor_reduce(mx[:], lg[:], AX, ALU.max).then_inc(route_step, 1)
                dve.wait_ge(route_step, s + 2)
                dve.tensor_tensor(lg[:], lg[:], mx[:].unsqueeze(2).broadcast_to([P, T, E0]), ALU.subtract)\
                   .then_inc(lg_ready, 1)
                dve.wait_ge(ex_ready, b + 1)
                dve.tensor_reduce(sm[:, 0, :], ex[:], AX, ALU.add).then_inc(route_step, 1)
                dve.wait_ge(route_step, s + 3)
                dve.reciprocal(sm[:, 1, :], sm[:, 0, :]).then_inc(route_step, 1)
                dve.wait_ge(route_step, s + 4)
                dve.tensor_tensor(pr[:], ex[:], sm[:, 1, :].unsqueeze(2).broadcast_to([P, T, E0]), ALU.mult)\
                   .then_inc(route_step, 1)
                dve.wait_ge(route_step, s + 5)
                own_wait(dve, mark_dve)
                for t in range(T):
                    ins = dve.max(top[:, t, :], pr[:, t, :])
                ins.then_inc(route_step, 1)
                dve.wait_ge(route_step, s + 6)
                own_wait(dve, mark_dve)
                for t in range(T):
                    ins = dve.max_index(idx[:, t, :], top[:, t, :], pr[:, t, :])
                ins.then_inc(route_step, 1)
                dve.wait_ge(route_step, s + 7)
                dve.tensor_copy(idf[:], idx[:, :, 0:2].rearrange("p t k -> p k t")).then_inc(route_step, 1)
                dve.tensor_copy(m["gate0"][:, bass.ds(b * 2 * T, 2 * T)].rearrange("p (k t) -> p k t", k=2),
                                top[:, :, 0:2].rearrange("p t k -> p k t"))
                dve.wait_ge(route_step, s + 8)
                iota = m["consts"][:, C_IOTA:C_IOTA + E0].unsqueeze(1).unsqueeze(1).broadcast_to([P, 2, T, E0])
                dve.tensor_tensor(oh[:], iota, idf[:].unsqueeze(3).broadcast_to([P, 2, T, E0]), ALU.is_equal)\
                   .then_inc(route_step, 1)
                dve.wait_ge(route_step, s + 9)
                dve.tensor_tensor(member[:, 0:T, :], oh[:, 0], oh[:, 1], ALU.add).then_inc(member_ready, 1)

            def route_rows(q, h):
                b = 2 * q + h
                s = ROUTE_STEPS * b
                dve.wait_ge(count_done, b + 1)
                dve.tensor_tensor(pos[:], count[:, 0:T, :], m["count0"][:].unsqueeze(1).broadcast_to([P, T, E0]),
                                  ALU.add).then_inc(route_step, 1)
                dve.wait_ge(route_step, s + 10)
                dve.tensor_tensor(m["count0"][:], m["count0"][:], count[:, T, :], ALU.add)
                dve.tensor_tensor(own[:], oh[:], pos[:].unsqueeze(1).broadcast_to([P, 2, T, E0]), ALU.mult)\
                   .then_inc(route_step, 1)
                dve.wait_ge(route_step, s + 11)
                dve.tensor_reduce(ownpos[:], own[:], AX, ALU.add).then_inc(route_step, 1)
                dve.wait_ge(route_step, s + 12)
                dve.scalar_tensor_tensor(out=rows[:, h], in0=idf[:], scalar=float(REGION), in1=ownpos[:],
                                         op0=ALU.mult, op1=ALU.add).then_inc(rows_ready, 1)
                dve.wait_ge(rows_ready, b + 1)
                dve.tensor_copy(m["slot0"][:, bass.ds(b * 2 * T, 2 * T)].rearrange("p (k t) -> p k t", k=2),
                                rows[:, h])

            def graph(q, h, first, last):
                b = 2 * q + h
                split_support(b, 0)
                if not last:
                    norm1_stats(q + h, 1 - h)
                split_layer(b, 0)
                if not last:
                    split_adj(b + 1, 1 - h, 0)
                split_support(b, 1)
                if not last:
                    norm1_apply(b + 1)
                split_layer(b, 1)
                if not last:
                    split_adj(b + 1, 1 - h, 1)
                split_support(b, 2)
                if not last:
                    split_in(b + 1)
                if not first:
                    route_choose(b - 1)
                residual_stats(q, h)
                if not first:
                    route_rows(q - 1 + h, 1 - h)
                norm2_apply(q, h)

            norm1_stats(0, 0)
            norm1_apply(0)
            dve.wait_ge(w_hi, 1)
            low_part(dve, wl[:], w[:], wh[:]).then_inc(w_lo, 1)
            split_adj(0, 0, 0)
            split_adj(0, 0, 1)
            split_in(0)
            pairs(dve, B, graph)
            route_choose(B - 1)
            route_rows(B // 2 - 1, 1)


def count_before(pe, m, count, member, done):
    pe.matmul(count[:], m["tri"][:], member[:], start=True, stop=False, skip_group_check=True)
    for t in range(T):
        mm = pe.matmul(count[:, t + 1:T + 1, :], m["ones"][:],
                       member[:, t:t + 1, :].broadcast_to([P, T - t, member.shape[2]]),
                       start=False, stop=(t == T - 1), skip_group_check=True)
    mm.then_inc(done, 1)


def moe0_phase(nc, a, m, sb):
    ident = m["ident"]
    with ExitStack() as ctx:
        def sem(name):
            return ctx.enter_context(nc.semaphore("b_" + name))

        mark_dve, mark_pool, mark_sp = sem("mark_dve"), sem("mark_pool"), sem("mark_sp")

        def psum(name, shape):
            return ctx.enter_context(nc.psum_tensor("b_" + name, shape, F32))

        w1 = sb(ctx, "b_w1", [P, KD * H0])
        zeros = sb(ctx, "b_zeros", [P, T * D])
        w2 = sb(ctx, "b_w2", [P, KH0 * D])
        w1h, w1l = sb(ctx, "b_w1h", [P, KD * H0], F32R), sb(ctx, "b_w1l", [P, KD * H0], F32R)
        w2h, w2l = sb(ctx, "b_w2h", [P, KH0 * D], F32R), sb(ctx, "b_w2l", [P, KH0 * D], F32R)
        b1 = sb(ctx, "b_b1", [P, 2, KH0])
        b2 = sb(ctx, "b_b2", [P, 2, D])
        xin = sb(ctx, "b_xin", [P, 2, T, D])
        xh, xl = sb(ctx, "b_xh", [P, KD, BLK], F32R), sb(ctx, "b_xl", [P, KD, BLK], F32R)
        ht = sb(ctx, "b_ht", [P, KH0, BLK])
        hh, hl = sb(ctx, "b_hh", [P, KH0, BLK], F32R), sb(ctx, "b_hl", [P, KH0, BLK], F32R)
        y = sb(ctx, "b_y", [P, 2, T, D])
        over = sb(ctx, "b_over", [P, E0, NTHR])
        blocks = sb(ctx, "b_blocks", [P, 3, E0])
        shift = sb(ctx, "b_shift", [P, 2, E0])
        beyond = sb(ctx, "b_beyond", [P, PAIRS, E0])
        moved = sb(ctx, "b_moved", [P, PAIRS])
        past = sb(ctx, "b_past", [1, 2, NBLK, E0])
        expert = sb(ctx, "b_expert", [1, 4, NBLK])
        tail = sb(ctx, "b_tail", [1, E0])
        table = sb(ctx, "b_table", [1, 2, NBLK], I32)
        tails = sb(ctx, "b_tails", [1, E0], I32)

        p_tr = psum("p_tr", [P, KD, BLK])
        p_h = psum("p_h", [P, KH0, BLK])
        p_y = psum("p_y", [P, T, D])

        rows_out = m["moe0_out"].rearrange("(j p t) d -> j p (t d)", p=P, t=T)
        step, table_ready, zeroed = sem("step"), sem("table"), sem("zeroed")
        s_tail = sem("tail")
        s_rows, s_bias = [sem("rows0"), sem("rows1")], [sem("bias0"), sem("bias1")]
        w1_in, w2_in = sem("w1_in"), sem("w2_in")
        w1h_ready, w1l_ready, w2h_ready, w2l_ready = sem("w1h"), sem("w1l"), sem("w2h"), sem("w2l")
        s_out = [sem("out0"), sem("out1")]
        tr_done, xh_ready, xl_ready, h_done = sem("tr_done"), sem("xh_ready"), sem("xl_ready"), sem("h_done")
        hh_ready, ht_ready, hl_ready = sem("hh_ready"), sem("ht_ready"), sem("hl_ready")
        y_done, y_ready = sem("y_done"), sem("y_ready")

        block = ctx.enter_context(nc.Block())

        @block.gpsimd
        def _(pool):
            pool.memset(zeros[:], 0.0).then_inc(zeroed, 1)

        @block.vector
        def _(dve):
            c0 = m["count0"]
            thr = m["consts"][:, C_THR:C_THR + NTHR]
            blk = m["consts"][0:1, C_BLK:C_BLK + NBLK]
            dve.tensor_tensor(over[:], c0[:].unsqueeze(2).broadcast_to([P, E0, NTHR]),
                              thr.unsqueeze(1).broadcast_to([P, E0, NTHR]), ALU.is_gt).then_inc(step, 1)
            dve.scalar_tensor_tensor(out=tails[:], in0=m["consts"][0:1, C_IOTA:C_IOTA + E0],
                                     scalar=float(REGION), in1=c0[0:1, :],
                                     op0=ALU.mult, op1=ALU.add).then_inc(table_ready, 1)
            dve.memset(blocks[:, 2, :], 1.0)
            dve.wait_ge(step, 1)
            dve.tensor_reduce(blocks[:, 0, :], over[:], AX, ALU.add).then_inc(step, 1)
            dve.wait_ge(step, 2)
            dve.tensor_tensor_scan(blocks[:, 1, :], blocks[:, 2, :], blocks[:, 0, :], 0.0, ALU.mult, ALU.add)\
               .then_inc(step, 1)
            dve.wait_ge(step, 3)
            dve.tensor_tensor(past[:, 0], blocks[0:1, 1, :].unsqueeze(1).broadcast_to([1, NBLK, E0]),
                              blk.unsqueeze(2).broadcast_to([1, NBLK, E0]), ALU.is_le).then_inc(step, 1)
            dve.wait_ge(step, 4)
            dve.tensor_tensor(past[:, 1], past[:, 0], blocks[0:1, 0, :].unsqueeze(1).broadcast_to([1, NBLK, E0]),
                              ALU.mult)
            dve.tensor_reduce(expert[:, 0, :], past[:, 0], AX, ALU.add).then_inc(step, 1)
            dve.wait_ge(step, 5)
            dve.tensor_reduce(expert[:, 1, :], past[:, 1], AX, ALU.add).then_inc(step, 1)
            dve.wait_ge(step, 6)
            dve.tensor_tensor(expert[:, 2, :], blk, expert[:, 1, :], ALU.subtract).then_inc(step, 1)
            dve.wait_ge(step, 7)
            dve.tensor_scalar(expert[:, 3, :], expert[:, 2, :], float(BLK), None, ALU.mult).then_inc(step, 1)
            dve.wait_ge(step, 8)
            dve.scalar_tensor_tensor(out=expert[:, 1, :], in0=expert[:, 0, :], scalar=float(REGION),
                                     in1=expert[:, 3, :], op0=ALU.mult, op1=ALU.add).then_inc(step, 1)
            dve.wait_ge(step, 9)
            dve.tensor_scalar(table[:, 0, :], expert[:, 1, :], float(SPARE), None, ALU.min)\
               .then_inc(table_ready, 1)
            dve.tensor_scalar(table[:, 1, :], expert[:, 0, :], float(E0 - 1), None, ALU.min)\
               .then_inc(table_ready, 1)
            dve.tensor_scalar(shift[:, 0, :], m["consts"][:, C_IOTA:C_IOTA + E0], float(REGION), None, ALU.mult)\
               .then_inc(step, 1)
            dve.tensor_scalar(shift[:, 1, 1:E0], blocks[:, 0, 0:E0 - 1], float(BLK), -float(REGION),
                              ALU.mult, ALU.add)
            dve.memset(shift[:, 1, 0:1], 0.0).then_inc(step, 1)
            dve.wait_ge(step, 11)
            dve.tensor_tensor(beyond[:], m["slot0"][:].unsqueeze(2).broadcast_to([P, PAIRS, E0]),
                              shift[:, 0, :].unsqueeze(1).broadcast_to([P, PAIRS, E0]), ALU.is_ge).then_inc(step, 1)
            dve.wait_ge(step, 12)
            dve.tensor_tensor(beyond[:], beyond[:], shift[:, 1, :].unsqueeze(1).broadcast_to([P, PAIRS, E0]),
                              ALU.mult).then_inc(step, 1)
            dve.wait_ge(step, 13)
            dve.tensor_reduce(moved[:], beyond[:], AX, ALU.add).then_inc(step, 1)
            dve.wait_ge(step, 14)
            dve.tensor_tensor(m["rows0"][:], m["slot0"][:], moved[:], ALU.add)

            def split_in(j):
                dve.wait_ge(xh_ready, j + 1)
                low_part(dve, xl[:], p_tr[:], xh[:]).then_inc(xl_ready, 1)
                dve.wait_ge(w1h_ready, j + 1)
                low_part(dve, w1l[:], w1[:], w1h[:]).then_inc(w1l_ready, 1)

            def one(q, h, first, last):
                j = 2 * q + h
                dve.wait_ge(w2h_ready, j + 1)
                low_part(dve, w2l[:], w2[:], w2h[:]).then_inc(w2l_ready, 1)
                for c in range(KH0):
                    dve.wait_ge(ht_ready, KH0 * j + c + 1)
                    low_part(dve, hl[:, c, :], ht[:, c, :], hh[:, c, :]).then_inc(hl_ready, 1)
                if not last:
                    split_in(j + 1)
                if not (isinstance(q, int) and q == 0):
                    dve.wait_ge(s_out[h], 16 * q)
                dve.wait_ge(s_bias[h], 32 * (q + 1))
                for c in range(TB):
                    dve.wait_ge(y_done, TB * j + c + 1)
                    dve.tensor_tensor(y[:, h, 2 * c:2 * c + 2, :], p_y[:, 2 * c:2 * c + 2, :],
                                      b2[:, h, :].unsqueeze(1).broadcast_to([P, 2, D]), ALU.add).then_inc(y_ready, 1)
            split_in(0)
            pairs(dve, NBLK, one)

        @block.sync
        def _(sp):
            sp.wait_ge(zeroed, 1)
            sp.wait_ge(table_ready, 3)
            for e in range(E0):
                row = sp.value_load(tails[0:1, e:e + 1], min_val=0, max_val=SPARE - BLK)
                sp.dma_start(m["moe0_in"][bass.ds(row, BLK), :].rearrange("(p t) d -> p (t d)", p=P),
                             zeros[:]).then_inc(s_tail, 16)

            def load_rows(q, h):
                row = sp.value_load(table[0:1, 0, bass.ds(2 * q + h, 1)], min_val=0, max_val=SPARE)
                sp.dma_start(xin[:, h].rearrange("p t d -> p (t d)"),
                             m["moe0_in"][bass.ds(row, BLK), :].rearrange("(p t) d -> p (t d)", p=P))\
                  .then_inc(s_rows[h], 16)

            def expert_of(j):
                return sp.value_load(table[0:1, 1, bass.ds(j, 1)], min_val=0, max_val=E0 - 1)

            def load(dst, src, e, done):
                sp.dma_start(dst, src[bass.ds(e, 1)].rearrange("e p c -> p (e c)")).then_inc(done, 16)

            def load_bias(e, h):
                load(b1[:, h, :], a["moe0_b1"], e, s_bias[h])
                sp.dma_start(b2[:, h, :], a["moe0_b2"][bass.ds(e, 1)].rearrange("e d -> (e d)").partition_broadcast(P))\
                  .then_inc(s_bias[h], 16)

            def one(q, h, first, last):
                j = 2 * q + h
                if not last:
                    sp.wait_ge(w1l_ready, j + 1)
                    own_wait(sp, mark_sp)
                    if not first:
                        sp.wait_ge(y_ready, TB * j)
                    own_wait(sp, mark_sp)
                    e = expert_of(j + 1)
                    load(w1[:], a["moe0_w1"], e, w1_in)
                    load_bias(e, 1 - h)
                    sp.wait_ge(w2l_ready, j + 1)
                    own_wait(sp, mark_sp)
                    load(w2[:], a["moe0_w2"], e, w2_in)
                if not (last or (h == 0 and isinstance(q, int) and q == NBLK // 2 - 1)):
                    sp.wait_ge(tr_done, j + 1)
                    own_wait(sp, mark_sp)
                    load_rows(q + 1, h)
                sp.wait_ge(y_ready, TB * j + TB)
                own_wait(sp, mark_sp)
                sp.dma_start(rows_out[j],
                             y[:, h].rearrange("p t d -> p (t d)")).then_inc(s_out[h], 16)
            e = expert_of(0)
            load(w1[:], a["moe0_w1"], e, w1_in)
            load_bias(e, 0)
            load(w2[:], a["moe0_w2"], e, w2_in)
            sp.wait_ge(s_tail, 16 * E0)
            own_wait(sp, mark_sp)
            load_rows(0, 0)
            load_rows(0, 1)
            pairs(sp, NBLK, one)
            for h in range(2):
                sp.wait_ge(s_out[h], 16 * (NBLK // 2))

        @block.tensor
        def _(pe):
            def turn(q, h):
                pe.wait_ge(s_rows[h], 16 * (q + 1))
                transposes(pe, p_tr, xin[:, h], ident, tr_done)

            def one(q, h, first, last):
                j = 2 * q + h
                pe.wait_ge(xl_ready, j + 1)
                pe.wait_ge(w1l_ready, j + 1)
                for c in range(KH0):
                    for k in range(KD):
                        col = slice(k * H0 + c * P, k * H0 + (c + 1) * P)
                        mm = exact(pe, p_h[:, c, :], (w1h[:, col], w1l[:, col]), (xh[:, k, :], xl[:, k, :]),
                                   k == 0, k == KD - 1)
                    mm.then_inc(h_done, 1)
                if not last:
                    turn(q + h, 1 - h)
                pe.wait_ge(w2l_ready, j + 1)
                for t in range(T):
                    tok = slice(t * P, (t + 1) * P)
                    if not first and t % 2 == 0:
                        pe.wait_ge(y_ready, TB * (j - 1) + t // 2 + 1)
                    for c in range(KH0):
                        if t == 0:
                            pe.wait_ge(hl_ready, KH0 * j + c + 1)
                        col = slice(c * D, (c + 1) * D)
                        mm = exact(pe, p_y[:, t, :], (hh[:, c, tok], hl[:, c, tok]), (w2h[:, col], w2l[:, col]),
                                   c == 0, c == KH0 - 1)
                    if t % 2:
                        mm.then_inc(y_done, 1)
            turn(0, 0)
            pairs(pe, NBLK, one)

        @block.scalar
        def _(act):
            def split_in(j):
                act.wait_ge(tr_done, j + 1)
                act.activation(xh[:], p_tr[:], ACT.Copy).then_inc(xh_ready, 1)
                act.wait_ge(w1_in, 16 * (j + 1))
                act.activation(w1h[:], w1[:], ACT.Copy).then_inc(w1h_ready, 1)

            def one(q, h, first, last):
                j = 2 * q + h
                act.wait_ge(w2_in, 16 * (j + 1))
                if not first:
                    act.wait_ge(y_done, TB * j)
                act.activation(w2h[:], w2[:], ACT.Copy).then_inc(w2h_ready, 1)
                act.wait_ge(s_bias[h], 32 * (q + 1))
                for c in range(KH0):
                    act.wait_ge(h_done, KH0 * j + c + 1)
                    act.activation(hh[:, c, :], p_h[:, c, :], ACT.Gelu, bias=b1[:, h, c:c + 1]).then_inc(hh_ready, 1)
                    act.activation(ht[:, c, :], p_h[:, c, :], ACT.Gelu, bias=b1[:, h, c:c + 1]).then_inc(ht_ready, 1)
                if not last:
                    split_in(j + 1)
            split_in(0)
            pairs(act, NBLK, one)


def attention_phase(nc, a, m, sb):
    x, adj, ident = m["x"], m["adj"], m["ident"]
    with ExitStack() as ctx:
        def sem(name):
            return ctx.enter_context(nc.semaphore("c_" + name))

        mark_dve, mark_pool, mark_sp = sem("mark_dve"), sem("mark_pool"), sem("mark_sp")

        def psum(name, shape):
            return ctx.enter_context(nc.psum_tensor("c_" + name, shape, F32))

        wp = sb(ctx, "c_wp", [P, KD, D])
        bpc = sb(ctx, "c_bpc", [P, GRP])
        bpr = sb(ctx, "c_bpr", [P, D])
        cd = sb(ctx, "c_cd", [P, GRP, P])
        cdh, cdl = sb(ctx, "c_cdh", [P, GRP, P], F32R), sb(ctx, "c_cdl", [P, GRP, P], F32R)
        wg = sb(ctx, "c_wg", [P, KD, E1])
        ws1, ws3 = sb(ctx, "c_ws1", [P, KD, HS]), sb(ctx, "c_ws3", [P, KD, HS])
        ws2 = sb(ctx, "c_ws2", [P, KHS, D])
        g = sb(ctx, "c_g", [P, 2 * T, D])
        grow = sb(ctx, "c_grow", [P, 2 * T], U32)
        ggate = sb(ctx, "c_ggate", [P, 2 * T])
        xn = sb(ctx, "c_xn", [P, T, D])
        xn3 = sb(ctx, "c_xn3", [P, 2, T, D])
        xt = sb(ctx, "c_xt", [P, KD, N])
        xt3 = sb(ctx, "c_xt3", [P, KD, N])
        st1, mv1, rs1 = sb(ctx, "c_st1", [P, T, 6]), sb(ctx, "c_mv1", [P, T, 2]), sb(ctx, "c_rs1", [P, T])
        st3, mv3, rs3 = sb(ctx, "c_st3", [P, T, 6]), sb(ctx, "c_mv3", [P, T, 2]), sb(ctx, "c_rs3", [P, T])
        xp = sb(ctx, "c_xp", [P, T, D])
        xpth, xptl = sb(ctx, "c_xpth", [P, GRP, N], F32R), sb(ctx, "c_xptl", [P, GRP, N], F32R)
        xcth, xctl = sb(ctx, "c_xcth", [P, HEADS, N], F32R), sb(ctx, "c_xctl", [P, HEADS, N], F32R)
        att = sb(ctx, "c_att", [P, 2, HG, N])
        ot = sb(ctx, "c_ot", [P, GRP, N])
        sh = sb(ctx, "c_sh", [P, KHS, N])
        sg = sb(ctx, "c_sg", [P, T, E1])
        top = sb(ctx, "c_top", [P, T, 8])
        idx = sb(ctx, "c_idx", [P, T, 8], U32)
        idf = sb(ctx, "c_idf", [P, 2, T])
        oh = sb(ctx, "c_oh", [P, 2, T, E1])
        member = sb(ctx, "c_member", [P, T + 1, E1], BF16)
        pos = sb(ctx, "c_pos", [P, T, E1])
        own = sb(ctx, "c_own", [P, 2, T, E1])
        ownpos = sb(ctx, "c_ownpos", [P, 2, T])
        fits = sb(ctx, "c_fits", [P, 2, T])
        inside = sb(ctx, "c_inside", [P, 2, T])
        srow = sb(ctx, "c_srow", [P, 2, T])
        gsum = sb(ctx, "c_gsum", [P, 2, T])
        gk = sb(ctx, "c_gk", [P, 2, T])
        rows = sb(ctx, "c_rows", [P, 2, 2, T], U32)

        p_s = psum("p_s", [P, HG, N])
        p_o = psum("p_o", [P, GRP, N])
        p_w = psum("p_w", [P, 2, 512])
        p_w_tok = p_w[:].rearrange("p a (c d) -> p (a c) d", d=D)
        p_s_tok = p_s[:, 0:2, :].rearrange("p a (c d) -> p (a c) d", d=D)
        logit = p_w[:, 0, 0:T * E1].rearrange("p (t e) -> p t e", t=T)
        count = p_w[:, 1, 0:(T + 1) * E1].rearrange("p (t e) -> p t e", t=T + 1)

        s_w, s_in, init = sem("w"), [sem("in0"), sem("in1")], sem("init")
        grow_ready, gathered, x2_step = sem("grow"), sem("gathered"), sem("x2_step")
        ln1_step, ln1_rs, xn_ready = sem("ln1_step"), sem("ln1_rs"), sem("xn_ready")
        ln3_step, ln3_rs, xn3_ready = sem("ln3_step"), sem("ln3_rs"), sem("xn3_ready")
        tr_done, xt_ready, tr3_done, xt3_ready = sem("tr_done"), sem("xt_ready"), sem("tr3_done"), sem("xt3_ready")
        xp_done, xp_ready = sem("xp_done"), sem("xp_ready")
        xpt_done, xpt_hi, xpt_lo = sem("xpt_done"), sem("xpt_hi"), sem("xpt_lo")
        cd_hi, cd_lo = sem("cd_hi"), sem("cd_lo")
        xct_done, xct_hi, xct_lo = sem("xct_done"), sem("xct_hi"), sem("xct_lo")
        s_done, prod_ready, att_ready, av_done = sem("s_done"), sem("prod_ready"), sem("att_ready"), sem("av_done")
        ot_ready, back_done, x3_ready = sem("ot_ready"), sem("back_done"), sem("x3_ready")
        log_done, sg_ready, sg_step = sem("log_done"), sem("sg_ready"), sem("sg_step")
        member_ready, count_done, rows_ready = sem("member"), sem("count_done"), sem("rows_ready")
        up_done, sh_ready, hs_ready = sem("up_done"), sem("sh_ready"), sem("hs_ready")
        down_done, x4_ready = sem("down_done"), sem("x4_ready")
        scattered = [sem("scattered0"), sem("scattered1")]
        UNITS = GRP * T
        NW = 8 + HEADS
        ROUTE_STEPS = 17

        block = ctx.enter_context(nc.Block())

        @block.sync
        def _(sp):
            for dst, name in ((wp[:], "wp"), (bpc[:], "bpc"), (wg[:], "wg"), (ws1[:], "ws1"),
                              (ws3[:], "ws3"), (ws2[:], "ws2")):
                sp.dma_start(dst, a[name]).then_inc(s_w, 16)
            sp.dma_start(bpr[:], a["bp"].partition_broadcast(P)).then_inc(s_w, 16)
            sp.wait_ge(init, 1)
            for i in range(HEADS):
                r = DH * (i % HG)
                sp.dma_start(cd[r:r + DH, i // HG, r:r + DH], a["ct"][i]).then_inc(s_w, 16)

            def graph(q, h, first, last):
                b = 2 * q + h
                if not (isinstance(q, int) and q == 0):
                    sp.wait_ge(prod_ready, 2 * UNITS * (b - 1))
                sp.dma_start(adj[:, h], a["adj"][b]).then_inc(s_in[h], 16)
            pairs(sp, B, graph)

        @block.gpsimd
        def _(pool):
            def gather(b):
                pool.wait_ge(grow_ready, b + 1)
                own_wait(pool, mark_pool)
                for i in range(2 * T):
                    pool.indirect_dma_start(
                        out=g[:, i, :], out_offset=None, in_=m["moe0_out"],
                        in_offset=bass.IndirectOffsetOnAxis(ap=grow[:, i:i + 1], axis=0)).then_inc(gathered, 16)

            def scale1(b):
                pool.wait_ge(ln1_step, 2 * b + 2)
                norm_scale(pool, mv1, m["half"], rs1, ln1_rs, 2 * b, mark_pool)

            def graph(q, h, first, last):
                b = 2 * q + h
                if not (last or (isinstance(q, int) and q == B // 2 - 1)):
                    gather(b + 2)
                if not last:
                    scale1(b + 1)
                pool.wait_ge(ln3_step, 2 * b + 2)
                norm_scale(pool, mv3, m["half"], rs3, ln3_rs, 2 * b, mark_pool)
                pool.wait_ge(rows_ready, b + 1)
                own_wait(pool, mark_pool)
                for k in range(2):
                    for t in range(T):
                        pool.indirect_dma_start(
                            out=m["moe1_in"], out_offset=bass.IndirectOffsetOnAxis(ap=rows[:, h, k, t:t + 1], axis=0),
                            in_=xn3[:, h, t, :], in_offset=None, bounds_check=E1 * CAP - 1, oob_is_err=False)\
                            .then_inc(scattered[h], 16)
            gather(0)
            scale1(0)
            gather(1)
            pairs(pool, B, graph)
            for h in range(2):
                pool.wait_ge(scattered[h], 16 * 2 * T * (B // 2))

        @block.tensor
        def _(pe):
            pe.wait_ge(s_w, 16 * (7 + HEADS))
            pe.wait_ge(init, 4)
            pe.wait_ge(cd_lo, 1)

            def project(b):
                pe.wait_ge(xn_ready, b + 1)
                transposes(pe, p_s[:, 0:2, :], xn, ident, tr_done)
                pe.wait_ge(xt_ready, b + 1)
                for t in range(T):
                    for k in range(KD):
                        mm = pe.matmul(p_s_tok[:, t, :], xt[:, k, t * P:(t + 1) * P], wp[:, k, :],
                                       start=(k == 0), stop=(k == KD - 1))
                    if t % 2:
                        mm.then_inc(xp_done, 1)
                for f in range(GRP):
                    for k in range(KD):
                        mm = pe.matmul(p_s[:, 2 + f, :], wp[:, k, f * P:(f + 1) * P], xt[:, k, :],
                                       start=(k == 0), stop=(k == KD - 1))
                    mm.then_inc(xpt_done, 1)

            def project_c(b):
                pe.wait_ge(xp_ready, TB * b + TB)
                for f in range(GRP):
                    pe.wait_ge(xpt_lo, GRP * b + f + 1)
                    exact(pe, p_s[:, f, :], (cdh[:, f, :], cdl[:, f, :]), (xpth[:, f, :], xptl[:, f, :]), True, True)\
                        .then_inc(xct_done, 1)

            def graph(q, h, first, last):
                b = 2 * q + h
                pe.wait_ge(xct_lo, HEADS * b + HEADS)

                def scores(u):
                    f, t = u // T, u % T
                    for i in range(HG):
                        if u > 0 and i % 2 == 0:
                            pe.wait_ge(prod_ready, 2 * (UNITS * b + u - 1) + i // 2 + 1)
                        tok, head = slice(t * P, (t + 1) * P), HG * f + i
                        mm = exact(pe, p_s[:, i, :], (xpth[:, f, tok], xptl[:, f, tok]),
                                   (xcth[:, head, :], xctl[:, head, :]), True, True)
                        if i % 2:
                            mm.then_inc(s_done, 1)

                def values(u):
                    f, t = u // T, u % T
                    pe.wait_ge(att_ready, 2 * (UNITS * b + u) + 2)
                    for i in range(HG):
                        c = DH * (HG * f + i)
                        mm = pe.matmul(p_o[DH * i:DH * i + DH, f, :], xp[:, t, c:c + DH], att[:, u % 2, i, :],
                                       start=(t == 0), stop=(t == T - 1))
                    mm.then_inc(av_done, 1)

                scores(0)
                for u in range(1, UNITS):
                    scores(u)
                    values(u - 1)
                values(UNITS - 1)
                if not first:
                    pe.wait_ge(x4_ready, TB * b)
                for f in range(GRP):
                    pe.wait_ge(ot_ready, GRP * b + f + 1)
                    for t in range(T):
                        mm = pe.transpose(p_w_tok[:, t, f * P:(f + 1) * P], ot[:, f, t * P:(t + 1) * P], ident)
                mm.then_inc(back_done, 1)
                if not last:
                    project(b + 1)
                pe.wait_ge(xn3_ready, b + 1)
                transposes(pe, p_w, xn3[:, h], ident, tr3_done)
                if not last:
                    project_c(b + 1)
                pe.wait_ge(xt3_ready, b + 1)
                for t in range(T):
                    for k in range(KD):
                        mm = pe.matmul(logit[:, t, :], xt3[:, k, t * P:(t + 1) * P], wg[:, k, :],
                                       start=(k == 0), stop=(k == KD - 1))
                mm.then_inc(log_done, 1)
                for c in range(KHS):
                    for k in range(KD):
                        pe.matmul(p_s[:, 2 + c, :], ws1[:, k, c * P:(c + 1) * P], xt3[:, k, :],
                                  start=(k == 0), stop=(k == KD - 1))
                    for k in range(KD):
                        mm = pe.matmul(p_o[:, c, :], ws3[:, k, c * P:(c + 1) * P], xt3[:, k, :],
                                       start=(k == 0), stop=(k == KD - 1))
                    mm.then_inc(up_done, 1)
                pe.wait_ge(member_ready, b + 1)
                count_before(pe, m, count, member, count_done)
                pe.wait_ge(sg_step, ROUTE_STEPS * b + 8)
                for t in range(T):
                    for c in range(KHS):
                        if t == 0:
                            pe.wait_ge(hs_ready, KHS * b + c + 1)
                        mm = pe.matmul(p_w_tok[:, t, :], sh[:, c, t * P:(t + 1) * P], ws2[:, c, :],
                                       start=(c == 0), stop=(c == KHS - 1))
                    if t % 2:
                        mm.then_inc(down_done, 1)
            project(0)
            project_c(0)
            pairs(pe, B, graph)

        @block.scalar
        def _(act):
            act.wait_ge(s_w, 16 * (7 + HEADS))
            act.wait_ge(init, 4)
            act.activation(cdh[:], cd[:], ACT.Copy).then_inc(cd_hi, 1)

            def evac_in(b):
                act.wait_ge(tr_done, b + 1)
                act.activation(xt[:], p_s[:, 0:2, :], ACT.Copy).then_inc(xt_ready, 1)
                for f in range(GRP):
                    act.wait_ge(xpt_done, GRP * b + f + 1)
                    act.activation(xpth[:, f, :], p_s[:, 2 + f, :], ACT.Identity, bias=bpc[:, f:f + 1])\
                       .then_inc(xpt_hi, 1)

            def evac_c(b, f):
                act.wait_ge(xct_done, GRP * b + f + 1)
                for i in range(HG):
                    r = slice(DH * i, DH * i + DH)
                    act.activation(xcth[r, HG * f + i, :], p_s[r, f, :], ACT.Copy).then_inc(xct_hi, 1)

            def graph(q, h, first, last):
                b = 2 * q + h
                for u in range(UNITS):
                    for i in range(2):
                        n = 2 * (UNITS * b + u) + i + 1
                        act.wait_ge(prod_ready, n)
                        part = att[:, u % 2, 2 * i:2 * i + 2, :]
                        act.activation(part, part, ACT.Tanh).then_inc(att_ready, 1)
                act.wait_ge(av_done, UNITS * b + UNITS)
                for f in range(GRP):
                    act.activation(ot[:, f, :], p_o[:, f, :], ACT.Relu).then_inc(ot_ready, 1)
                if not last:
                    evac_in(b + 1)
                act.wait_ge(tr3_done, b + 1)
                act.activation(xt3[:], p_w[:], ACT.Copy).then_inc(xt3_ready, 1)
                if not last:
                    evac_c(b + 1, 0)
                act.wait_ge(log_done, b + 1)
                act.activation(sg[:], logit, ACT.Exp, scale=-1.0).then_inc(sg_ready, 1)
                for c in range(KHS):
                    act.wait_ge(up_done, KHS * b + c + 1)
                    act.activation(sh[:, c, :], p_s[:, 2 + c, :], ACT.Silu).then_inc(sh_ready, 1)
                if not last:
                    evac_c(b + 1, 1)
            evac_in(0)
            evac_c(0, 0)
            evac_c(0, 1)
            pairs(act, B, graph)

        @block.vector
        def _(dve):
            def fetch(b):
                dve.tensor_copy(ggate[:], m["gate0"][:, bass.ds(b * 2 * T, 2 * T)])
                dve.tensor_copy(grow[:], m["rows0"][:, bass.ds(b * 2 * T, 2 * T)]).then_inc(grow_ready, 1)

            fetch(0)
            dve.memset(cd[:], 0.0).then_inc(init, 1)
            dve.memset(xcth[:].bitcast(F32), 0.0).then_inc(init, 1)
            dve.memset(xctl[:].bitcast(F32), 0.0).then_inc(init, 1)
            dve.memset(member[:], 0.0).then_inc(init, 1)
            dve.wait_ge(s_w, 16 * (7 + HEADS))

            def add_moe0(b, fetch_next):
                dve.wait_ge(gathered, 16 * 2 * T * (b + 1))
                dve.wait_ge(grow_ready, b + 1)
                for k in range(2):
                    for t in range(T):
                        if k == 1:
                            dve.wait_ge(x2_step, 2 * T * b + t + 1)
                        dve.scalar_tensor_tensor(out=x[:, b * T + t, :], in0=g[:, k * T + t, :],
                                                 scalar=ggate[:, k * T + t:k * T + t + 1],
                                                 in1=x[:, b * T + t, :], op0=ALU.mult, op1=ALU.add)\
                           .then_inc(x2_step, 1)
                dve.wait_ge(x2_step, 2 * T * (b + 1))
                if fetch_next:
                    fetch(b + 1)

            def norm1_apply(b):
                dve.wait_ge(ln1_rs, 2 * b + 2)
                norm_apply(dve, x, b, mv1, rs1, xn, xn_ready)

            def evac_projection(b):
                for c in range(TB):
                    dve.wait_ge(xp_done, TB * b + c + 1)
                    dve.tensor_tensor(xp[:, 2 * c:2 * c + 2, :], p_s_tok[:, 2 * c:2 * c + 2, :],
                                      bpr[:].unsqueeze(1).broadcast_to([P, 2, D]), ALU.add).then_inc(xp_ready, 1)

            def split_projection(b):
                for f in range(GRP):
                    dve.wait_ge(xpt_hi, GRP * b + f + 1)
                    dve.scalar_tensor_tensor(out=xptl[:, f, :], in0=p_s[:, 2 + f, :], scalar=bpc[:, f:f + 1],
                                             in1=xpth[:, f, :].bitcast(F32), op0=ALU.add, op1=ALU.subtract)\
                       .then_inc(xpt_lo, 1)

            def split_c(b, f):
                for i in range(HG):
                    r = slice(DH * i, DH * i + DH)
                    dve.wait_ge(xct_hi, HEADS * b + HG * f + i + 1)
                    low_part(dve, xctl[r, HG * f + i, :], p_s[r, f, :], xcth[r, HG * f + i, :]).then_inc(xct_lo, 1)

            dve.wait_ge(cd_hi, 1)
            low_part(dve, cdl[:], cd[:], cdh[:]).then_inc(cd_lo, 1)
            add_moe0(0, True)
            norm_stats(dve, x, 0, st1, mv1, ln1_step, 0, mark_dve)
            norm1_apply(0)
            evac_projection(0)
            split_projection(0)
            split_c(0, 0)
            split_c(0, 1)

            def graph(q, h, first, last):
                b = 2 * q + h
                dve.wait_ge(s_in[h], 16 * (q + 1))
                for u in range(UNITS):
                    t = u % T
                    if u >= 2:
                        dve.wait_ge(av_done, UNITS * b + u - 1)
                    for i in range(2):
                        dve.wait_ge(s_done, 2 * (UNITS * b + u) + i + 1)
                        ins = dve.tensor_tensor(att[:, u % 2, 2 * i:2 * i + 2, :], p_s[:, 2 * i:2 * i + 2, :],
                                                adj[:, h, t, :].unsqueeze(1).broadcast_to([P, 2, N]), ALU.mult)
                        ins.then_inc(prod_ready, 1)
                    if u == 1 and not last:
                        add_moe0(b + 1, not (isinstance(q, int) and q == B // 2 - 1))
                    if u == 3 and not last:
                        norm_stats(dve, x, b + 1, st1, mv1, ln1_step, 2 * (b + 1), mark_dve)
                    if u == 5 and not last:
                        norm1_apply(b + 1)
                dve.wait_ge(back_done, b + 1)
                xb = x[:, bass.ds(b * T, T), :]
                dve.tensor_tensor(xb, xb, p_w_tok, ALU.add).then_inc(x3_ready, 1)
                dve.wait_ge(x3_ready, b + 1)
                if not (isinstance(q, int) and q == 0):
                    dve.wait_ge(scattered[h], 16 * 2 * T * q)
                norm_stats(dve, x, b, st3, mv3, ln3_step, 2 * b, mark_dve)
                dve.wait_ge(ln3_rs, 2 * b + 2)
                norm_apply(dve, x, b, mv3, rs3, xn3[:, h], xn3_ready)
                if not last:
                    evac_projection(b + 1)
                    split_projection(b + 1)
                    split_c(b + 1, 0)
                s = ROUTE_STEPS * b
                dve.wait_ge(sg_ready, b + 1)
                dve.tensor_scalar(sg[:], sg[:], 1.0, None, ALU.add).then_inc(sg_step, 1)
                dve.wait_ge(sg_step, s + 1)
                dve.reciprocal(sg[:], sg[:]).then_inc(sg_step, 1)
                dve.wait_ge(sg_step, s + 2)
                own_wait(dve, mark_dve)
                for t in range(T):
                    ins = dve.max(top[:, t, :], sg[:, t, :])
                ins.then_inc(sg_step, 1)
                dve.wait_ge(sg_step, s + 3)
                own_wait(dve, mark_dve)
                for t in range(T):
                    ins = dve.max_index(idx[:, t, :], top[:, t, :], sg[:, t, :])
                ins.then_inc(sg_step, 1)
                dve.wait_ge(sg_step, s + 4)
                dve.tensor_copy(idf[:], idx[:, :, 0:2].rearrange("p t k -> p k t")).then_inc(sg_step, 1)
                dve.wait_ge(sg_step, s + 5)
                iota = m["consts"][:, C_IOTA:C_IOTA + E1].unsqueeze(1).broadcast_to([P, T, E1])
                for k in range(2):
                    ins = dve.tensor_tensor(oh[:, k], iota, idf[:, k, :].unsqueeze(2).broadcast_to([P, T, E1]),
                                            ALU.is_equal)
                ins.then_inc(sg_step, 1)
                dve.wait_ge(sg_step, s + 6)
                dve.tensor_tensor(member[:, 0:T, :], oh[:, 0], oh[:, 1], ALU.add).then_inc(member_ready, 1)
                for c in range(KHS):
                    dve.wait_ge(sh_ready, KHS * b + c + 1)
                    dve.tensor_tensor(sh[:, c, :], sh[:, c, :], p_o[:, c, :], ALU.mult).then_inc(hs_ready, 1)
                dve.wait_ge(count_done, b + 1)
                dve.tensor_tensor(pos[:], count[:, 0:T, :], m["count1"][:].unsqueeze(1).broadcast_to([P, T, E1]),
                                  ALU.add).then_inc(sg_step, 1)
                dve.wait_ge(sg_step, s + 7)
                dve.tensor_tensor(m["count1"][:], m["count1"][:], count[:, T, :], ALU.add)
                for k in range(2):
                    ins = dve.tensor_tensor(own[:, k], oh[:, k], pos[:], ALU.mult)
                ins.then_inc(sg_step, 1)
                if not last:
                    split_c(b + 1, 1)
                dve.wait_ge(sg_step, s + 8)
                dve.tensor_reduce(ownpos[:], own[:], AX, ALU.add).then_inc(sg_step, 1)
                dve.wait_ge(sg_step, s + 9)
                dve.tensor_scalar(fits[:], ownpos[:], float(CAP), None, ALU.is_lt).then_inc(sg_step, 1)
                dve.tensor_scalar(srow[:], ownpos[:], float(CAP), SKIP, ALU.is_ge, ALU.mult)
                dve.tensor_scalar(inside[:], ownpos[:], float(CAP - 1), None, ALU.min)
                dve.tensor_tensor(gsum[:, 0, :], top[:, :, 0], top[:, :, 1], ALU.add).then_inc(sg_step, 1)
                dve.wait_ge(sg_step, s + 11)
                dve.tensor_scalar(gsum[:, 1, :], gsum[:, 0, :], 1e-20, None, ALU.add).then_inc(sg_step, 1)
                dve.tensor_tensor(srow[:], srow[:], ownpos[:], ALU.add)
                dve.wait_ge(sg_step, s + 12)
                dve.reciprocal(gsum[:, 0, :], gsum[:, 1, :]).then_inc(sg_step, 1)
                dve.wait_ge(sg_step, s + 13)
                dve.tensor_tensor(gk[:], top[:, :, 0:2].rearrange("p t k -> p k t"),
                                  gsum[:, 0, :].unsqueeze(1).broadcast_to([P, 2, T]), ALU.mult).then_inc(sg_step, 1)
                dve.wait_ge(sg_step, s + 14)
                dve.scalar_tensor_tensor(out=gk[:], in0=gk[:], scalar=ROUTE_SCALE, in1=fits[:],
                                         op0=ALU.mult, op1=ALU.mult).then_inc(sg_step, 1)
                dve.scalar_tensor_tensor(out=rows[:, h], in0=idf[:], scalar=float(CAP), in1=srow[:],
                                         op0=ALU.mult, op1=ALU.add).then_inc(rows_ready, 1)
                dve.scalar_tensor_tensor(out=m["rows1"][:, bass.ds(b * 2 * T, 2 * T)].rearrange("p (k t) -> p k t", k=2),
                                         in0=idf[:], scalar=float(CAP), in1=inside[:],
                                         op0=ALU.mult, op1=ALU.add).then_inc(sg_step, 1)
                dve.wait_ge(sg_step, s + 16)
                dve.tensor_copy(m["gate1"][:, bass.ds(b * 2 * T, 2 * T)].rearrange("p (k t) -> p k t", k=2), gk[:])\
                   .then_inc(sg_step, 1)
                for c in range(TB):
                    dve.wait_ge(down_done, TB * b + c + 1)
                    xc = x[:, bass.ds(b * T + 2 * c, 2), :]
                    dve.tensor_tensor(xc, xc, p_w_tok[:, 2 * c:2 * c + 2, :], ALU.add).then_inc(x4_ready, 1)
            pairs(dve, B, graph)


def moe1_phase(nc, a, m, sb):
    ident = m["ident"]
    with ExitStack() as ctx:
        def sem(name):
            return ctx.enter_context(nc.semaphore("d_" + name))

        mark_dve, mark_pool, mark_sp = sem("mark_dve"), sem("mark_pool"), sem("mark_sp")

        def psum(name, shape):
            return ctx.enter_context(nc.psum_tensor("d_" + name, shape, F32))

        w = sb(ctx, "d_w", [P, 2, W_END1])
        wh, wl = sb(ctx, "d_wh", [P, 2, W_END1], F32R), sb(ctx, "d_wl", [P, 2, W_END1], F32R)
        xin = sb(ctx, "d_xin", [P, 2, T, D])
        xh, xl = sb(ctx, "d_xh", [P, 2, KD, CAP], F32R), sb(ctx, "d_xl", [P, 2, KD, CAP], F32R)
        gate = sb(ctx, "d_gate", [P, CAP])
        ht = sb(ctx, "d_ht", [P, 2, CAP])
        hh, hl = sb(ctx, "d_hh", [P, 2, CAP], F32R), sb(ctx, "d_hl", [P, 2, CAP], F32R)
        y = sb(ctx, "d_y", [P, 2, T, D])
        p_tr = psum("p_tr", [P, KD, CAP])
        p_h = psum("p_h", [P, 2, 2, CAP])
        p_y = psum("p_y", [P, T, D])
        s_rows, s_up = [sem("rows0"), sem("rows1")], [sem("up0"), sem("up1")]
        s_down = [sem("down0"), sem("down1")]
        s_out = [sem("out0"), sem("out1")]
        tr_done, xh_ready, xl_ready, up_done = sem("tr_done"), sem("xh_ready"), sem("xl_ready"), sem("up_done")
        uph_ready, upl_ready = sem("uph_ready"), sem("upl_ready")
        downh_ready, downl_ready = sem("downh_ready"), sem("downl_ready")
        gate_ready, ht_ready, hh_ready, hl_ready = sem("gate_ready"), sem("ht_ready"), sem("hh_ready"), sem("hl_ready")
        y_done, y_ready = sem("y_done"), sem("y_ready")
        rows_in = m["moe1_in"].rearrange("(e p t) d -> e p (t d)", p=P, t=T)
        rows_out = m["moe1_out"].rearrange("(e p t) d -> e p (t d)", p=P, t=T)
        up, dn = slice(0, W2_1), slice(W2_1, W_END1)

        def at_start(q):
            return isinstance(q, int) and q == 0

        block = ctx.enter_context(nc.Block())

        @block.sync
        def _(sp):
            def load_rows(q, h):
                sp.dma_start(xin[:, h].rearrange("p t d -> p (t d)"), rows_in[2 * q + h]).then_inc(s_rows[h], 16)

            def load_up(q, h):
                sp.dma_start(w[:, h, up], a["moe1_w"][2 * q + h][:, up]).then_inc(s_up[h], 16)

            def load_down(q, h):
                sp.dma_start(w[:, h, dn], a["moe1_w"][2 * q + h][:, dn]).then_inc(s_down[h], 16)

            def store(q, h):
                e = 2 * q + h
                sp.wait_ge(y_ready, TB * e + TB)
                sp.dma_start(rows_out[e], y[:, h].rearrange("p t d -> p (t d)")).then_inc(s_out[h], 16)

            def one(q, h, first, last):
                e = 2 * q + h
                if not (isinstance(q, int) and q == E1 // 2 - 1):
                    sp.wait_ge(tr_done, e + 1)
                    load_rows(q + 1, h)
                    sp.wait_ge(upl_ready, e + 1)
                    load_up(q + 1, h)
                if not (first or last):
                    sp.wait_ge(downl_ready, e)
                    load_down(q + h, 1 - h)
                if not at_start(q):
                    store(q - 1, h)
            for h in range(2):
                sp.sem_inc(s_out[h], 1)
            for h in range(2):
                load_rows(0, h)
                load_up(0, h)
                load_down(0, h)
            pairs(sp, E1, one)
            for h in range(2):
                store(E1 // 2 - 1, h)
            for h in range(2):
                sp.wait_ge(s_out[h], 16 * (E1 // 2) + 1)

        @block.tensor
        def _(pe):
            def turn(q, h):
                pe.wait_ge(s_rows[h], 16 * (q + 1))
                transposes(pe, p_tr, xin[:, h], ident, tr_done)

            def down(q, h):
                e = 2 * q + h
                pe.wait_ge(downl_ready, e + 1)
                pe.wait_ge(hl_ready, e + 1)
                for t in range(T):
                    tok = slice(t * P, (t + 1) * P)
                    if not (at_start(q) and h == 0) and t % 2 == 0:
                        pe.wait_ge(y_ready, TB * (e - 1) + t // 2 + 1)
                    mm = exact(pe, p_y[:, t, :], (hh[:, h, tok], hl[:, h, tok]), (wh[:, h, dn], wl[:, h, dn]),
                               True, True)
                    if t % 2:
                        mm.then_inc(y_done, 1)

            def one(q, h, first, last):
                e = 2 * q + h
                pe.wait_ge(xl_ready, e + 1)
                if not last:
                    turn(q + h, 1 - h)
                pe.wait_ge(upl_ready, e + 1)
                for i, start in enumerate((W1_1, W3_1)):
                    for k in range(KD):
                        col = slice(start + k * H1, start + (k + 1) * H1)
                        mm = exact(pe, p_h[:, h, i, :], (wh[:, h, col], wl[:, h, col]),
                                   (xh[:, h, k, :], xl[:, h, k, :]), k == 0, k == KD - 1)
                    mm.then_inc(up_done, 1)
                if not first:
                    down(q - 1 + h, 1 - h)
            turn(0, 0)
            pairs(pe, E1, one)
            down(E1 // 2 - 1, 1)

        @block.scalar
        def _(act):
            def split_in(q, h):
                e = 2 * q + h
                act.wait_ge(tr_done, e + 1)
                act.activation(xh[:, h], p_tr[:], ACT.Copy).then_inc(xh_ready, 1)
                act.wait_ge(s_up[h], 16 * (q + 1))
                act.activation(wh[:, h, up], w[:, h, up], ACT.Copy).then_inc(uph_ready, 1)

            def one(q, h, first, last):
                e = 2 * q + h
                if not last:
                    split_in(q + h, 1 - h)
                if not at_start(q):
                    act.wait_ge(y_done, TB * (e - 1))
                act.wait_ge(s_down[h], 16 * (q + 1))
                act.activation(wh[:, h, dn], w[:, h, dn], ACT.Copy).then_inc(downh_ready, 1)
                act.wait_ge(up_done, 2 * e + 1)
                act.activation(gate[:], p_h[:, h, 0, :], ACT.Silu).then_inc(gate_ready, 1)
                act.wait_ge(ht_ready, e + 1)
                act.activation(hh[:, h, :], ht[:, h], ACT.Copy).then_inc(hh_ready, 1)
            split_in(0, 0)
            pairs(act, E1, one)

        @block.gpsimd
        def _(pool):
            def split_up(q, h):
                pool.wait_ge(uph_ready, 2 * q + h + 1)
                own_wait(pool, mark_pool)
                low_part(pool, wl[:, h, up], w[:, h, up], wh[:, h, up]).then_inc(upl_ready, 1)

            def one(q, h, first, last):
                if not last:
                    split_up(q + h, 1 - h)
                pool.wait_ge(downh_ready, 2 * q + h + 1)
                own_wait(pool, mark_pool)
                low_part(pool, wl[:, h, dn], w[:, h, dn], wh[:, h, dn]).then_inc(downl_ready, 1)
            split_up(0, 0)
            pairs(pool, E1, one)

        @block.vector
        def _(dve):
            def split_rows(q, h):
                dve.wait_ge(xh_ready, 2 * q + h + 1)
                low_part(dve, xl[:, h], p_tr[:], xh[:, h]).then_inc(xl_ready, 1)

            def result(q, h, c):
                e = 2 * q + h
                dve.wait_ge(y_done, TB * e + c + 1)
                dve.tensor_copy(y[:, h, 2 * c:2 * c + 2, :], p_y[:, 2 * c:2 * c + 2, :]).then_inc(y_ready, 1)

            def one(q, h, first, last):
                e = 2 * q + h
                if not last:
                    split_rows(q + h, 1 - h)
                dve.wait_ge(gate_ready, e + 1)
                dve.wait_ge(up_done, 2 * e + 2)
                dve.tensor_tensor(ht[:, h], gate[:], p_h[:, h, 1, :], ALU.mult).then_inc(ht_ready, 1)
                if not first:
                    if not at_start(q):
                        dve.wait_ge(s_out[1 - h], 16 * (q - 1 + h) + 1)
                    result(q - 1 + h, 1 - h, 0)
                dve.wait_ge(hh_ready, e + 1)
                low_part(dve, hl[:, h, :], ht[:, h], hh[:, h, :]).then_inc(hl_ready, 1)
                if not first:
                    result(q - 1 + h, 1 - h, 1)
            split_rows(0, 0)
            pairs(dve, E1, one)
            dve.wait_ge(s_out[1], 16 * (E1 // 2 - 1) + 1)
            for c in range(TB):
                result(E1 // 2 - 1, 1, c)


def combine_phase(nc, a, m, sb, out):
    x = m["x"]
    with ExitStack() as ctx:
        def sem(name):
            return ctx.enter_context(nc.semaphore("e_" + name))

        mark_dve, mark_pool, mark_sp = sem("mark_dve"), sem("mark_pool"), sem("mark_sp")

        g = sb(ctx, "e_g", [P, 2, 2 * T, D])
        grow = sb(ctx, "e_grow", [P, 2, 2 * T], U32)
        ggate = sb(ctx, "e_ggate", [P, 2, 2 * T])
        grow_ready, step, s_out = sem("grow"), sem("step"), sem("out")
        gathered = [sem("gathered0"), sem("gathered1")]
        block = ctx.enter_context(nc.Block())

        @block.gpsimd
        def _(pool):
            def graph(q, h, first, last):
                b = 2 * q + h
                pool.wait_ge(grow_ready, b + 1)
                own_wait(pool, mark_pool)
                for i in range(2 * T):
                    pool.indirect_dma_start(
                        out=g[:, h, i, :], out_offset=None, in_=m["moe1_out"],
                        in_offset=bass.IndirectOffsetOnAxis(ap=grow[:, h, i:i + 1], axis=0)).then_inc(gathered[h], 16)
            pairs(pool, B, graph)

        @block.vector
        def _(dve):
            def fetch(q, h):
                b = 2 * q + h
                dve.tensor_copy(ggate[:, h, :], m["gate1"][:, bass.ds(b * 2 * T, 2 * T)])
                dve.tensor_copy(grow[:, h, :], m["rows1"][:, bass.ds(b * 2 * T, 2 * T)]).then_inc(grow_ready, 1)

            fetch(0, 0)

            def graph(q, h, first, last):
                b = 2 * q + h
                if not last:
                    fetch(q + h, 1 - h)
                dve.wait_ge(grow_ready, b + 1)
                dve.wait_ge(gathered[h], 16 * 2 * T * (q + 1))
                for k in range(2):
                    for t in range(T):
                        if k == 1:
                            dve.wait_ge(step, 2 * T * b + t + 1)
                        dve.scalar_tensor_tensor(out=x[:, b * T + t, :], in0=g[:, h, k * T + t, :],
                                                 scalar=ggate[:, h, k * T + t:k * T + t + 1],
                                                 in1=x[:, b * T + t, :], op0=ALU.mult, op1=ALU.add)\
                           .then_inc(step, 1)
                dve.wait_ge(step, 2 * T * (b + 1))
            pairs(dve, B, graph)

        @block.sync
        def _(sp):
            def graph(q, h, first, last):
                b = 2 * q + h
                sp.wait_ge(step, 2 * T * (b + 1))
                sp.dma_start(out[:, bass.ds(b * T, T), :], x[:, bass.ds(b * T, T), :]).then_inc(s_out, 16)
            pairs(sp, B, graph)
            sp.wait_ge(s_out, 16 * B)


def by_rows(w, k):
    return np.ascontiguousarray(w.reshape(k, P, -1).transpose(1, 0, 2))


def kernel(x, adj, L0_gnn_W1, L0_gnn_b1, L0_gnn_W2, L0_gnn_b2, L0_gnn_W3, L0_gnn_b3, L0_ffn_Wr, L0_ffn_br,
           L0_ffn_W1, L0_ffn_b1, L0_ffn_W2, L0_ffn_b2, L1_gnn_Wp, L1_gnn_bp, L1_gnn_C, L1_ffn_gate_w,
           L1_ffn_w1, L1_ffn_w3, L1_ffn_w2, L1_ffn_sw1, L1_ffn_sw3, L1_ffn_sw2):
    import concourse.bacc as bacc
    from concourse.bass_utils import run_bass_kernel_spmd

    flat = lambda w: w.reshape(w.shape[0], P, -1)
    consts = np.zeros((P, C_END), np.float32)
    consts[:, C_ID:C_ID + P] = np.eye(P)
    consts[:, C_TRI:C_TRI + P] = np.triu(np.ones((P, P)), 1)
    consts[:, C_ONE:C_ONE + P] = 1
    consts[:, C_IOTA:C_IOTA + E1] = np.arange(E1)
    consts[:, C_THR:C_THR + NTHR] = np.arange(NTHR) * BLK
    consts[:, C_BLK:C_BLK + NBLK] = np.arange(NBLK)
    rows = lambda w, k: w.reshape(w.shape[0], k, P, -1).transpose(0, 2, 1, 3).reshape(w.shape[0], P, -1)
    ins = {
        "consts": consts,
        "x": x.reshape(B * T, P, D).transpose(1, 0, 2),
        "adj": adj.transpose(0, 2, 1).reshape(B, T, P, N).transpose(0, 2, 1, 3),
        "w1": by_rows(L0_gnn_W1, KD), "w2": by_rows(L0_gnn_W2, KD), "w3": by_rows(L0_gnn_W3, KD),
        "b1": L0_gnn_b1.reshape(KD, P).T, "b2": L0_gnn_b2.reshape(KD, P).T, "b3": L0_gnn_b3,
        "wr": by_rows(L0_ffn_Wr.T, KD), "br": L0_ffn_br,
        "moe0_w1": rows(L0_ffn_W1, KD), "moe0_w2": rows(L0_ffn_W2, KH0),
        "moe0_b1": L0_ffn_b1.reshape(E0, KH0, P).transpose(0, 2, 1),
        "moe0_b2": L0_ffn_b2,
        "wp": by_rows(L1_gnn_Wp.transpose(1, 0, 2).reshape(D, HEADS * DH), KD),
        "bp": L1_gnn_bp.reshape(HEADS * DH), "bpc": L1_gnn_bp.reshape(GRP, P).T,
        "ct": L1_gnn_C.transpose(0, 2, 1),
        "wg": by_rows(L1_ffn_gate_w.T, KD),
        "ws1": by_rows(L1_ffn_sw1, KD), "ws3": by_rows(L1_ffn_sw3, KD), "ws2": by_rows(L1_ffn_sw2, KHS),
        "moe1_w": np.concatenate([rows(L1_ffn_w1, KD), rows(L1_ffn_w3, KD), L1_ffn_w2], axis=2),
    }
    ins = {k: np.ascontiguousarray(v) for k, v in ins.items()}
    nc = bacc.Bacc("TRN2", target_bir_lowering=False, num_devices=1)
    a = {k: nc.dram_tensor(f"in_{k}", v.shape, mybir.dt.from_np(v.dtype), kind="ExternalInput").ap()
         for k, v in ins.items()}
    out = nc.dram_tensor("out_x", (P, B * T, D), F32, kind="ExternalOutput").ap()
    build(nc, a, out)
    r = run_bass_kernel_spmd(nc, [{f"in_{k}": v for k, v in ins.items()}], core_ids=[0])
    return np.ascontiguousarray(r.results[0]["out_x"].transpose(1, 0, 2)).reshape(B, N, D)
```
